# Optimizing a Trainium2 kernel written in Bass

```python
import numpy as np
import jax
import jax.numpy as jnp

def _softmax(x, axis=-1):
    return jax.nn.softmax(x, axis=axis)

def _gelu(x):
    return jax.nn.gelu(x, approximate=True)

def _silu(x):
    return jax.nn.silu(x)

def _sigmoid(x):
    return jax.nn.sigmoid(x)

def _layernorm(x, axis=-1, eps=1e-05):
    m = jnp.mean(x, axis=axis, keepdims=True)
    v = jnp.var(x, axis=axis, keepdims=True)
    return (x - m) / jnp.sqrt(v + eps)

def _scatter_add(tgt, idx, src, axis=0):
    return tgt.at[idx].add(src)

def _segment_sum(src, seg, n):
    return jax.ops.segment_sum(src, seg, n)
kernel_name = 'mk_adaln_d1_jaxref_r8_2445a7'

def setup_inputs(seed: int=0):
    np.random.seed(seed)
    _w = jnp.asarray

    def _L0_attn_setup():
        import jax, jax.numpy as jnp
        import numpy as np
        EPS = 1e-15
        HEAD_DIM = 32
        PAD_VAL = 1.0
        key = jax.random.key(seed)
        k1, k2, k3, k4 = jax.random.split(key, 4)
        B, N, C = (2, 512, 256)
        s = 1.0 / np.sqrt(C).astype(np.float32)
        x = jax.random.normal(k1, (B, N, C), jnp.float32)
        w_qkv = jax.random.normal(k2, (3 * C, C), jnp.float32) * s
        w_proj = jax.random.normal(k3, (C, C), jnp.float32) * s
        b_proj = jax.random.normal(k4, (C,), jnp.float32) * 0.01
        return {'x': x, 'w_qkv': w_qkv, 'w_proj': w_proj, 'b_proj': b_proj}
    _L0_attn_in = _L0_attn_setup()

    def _L0_ffn_setup():
        import jax, jax.numpy as jnp
        import numpy as np
        H = 256
        M = 176
        E = 32
        TOPK = 6
        G = 8
        TOPK_G = 4
        SH = 2
        B, S = (1, 128)
        key = jax.random.key(seed)
        ks = jax.random.split(key, 9)
        sc = 0.02
        return {'x': jax.random.normal(ks[0], (B, S, H), dtype=jnp.float32), 'w_router': jax.random.normal(ks[1], (H, E), dtype=jnp.float32) * sc, 'corr_bias': jax.random.normal(ks[2], (E,), dtype=jnp.float32) * 0.1, 'gate_w': jax.random.normal(ks[3], (E, H, M), dtype=jnp.float32) * sc, 'up_w': jax.random.normal(ks[4], (E, H, M), dtype=jnp.float32) * sc, 'down_w': jax.random.normal(ks[5], (E, M, H), dtype=jnp.float32) * sc, 'sh_gate_w': jax.random.normal(ks[6], (H, M * SH), dtype=jnp.float32) * sc, 'sh_up_w': jax.random.normal(ks[7], (H, M * SH), dtype=jnp.float32) * sc, 'sh_down_w': jax.random.normal(ks[8], (M * SH, H), dtype=jnp.float32) * sc}
    _L0_ffn_in = _L0_ffn_setup()
    _L0_c = _w((lambda *s: np.random.randn(*s).astype(np.float32) * 0.05)(2, 256))
    _L0_wmod = _w((lambda *s: np.random.randn(*s).astype(np.float32) * 0.05)(256, 6 * 256) * 256 ** (-0.5))
    _d = {'L0_attn_x': _L0_attn_in['x'], 'L0_attn_w_qkv': _L0_attn_in['w_qkv'], 'L0_attn_w_proj': _L0_attn_in['w_proj'], 'L0_attn_b_proj': _L0_attn_in['b_proj'], 'L0_ffn_w_router': _L0_ffn_in['w_router'], 'L0_ffn_corr_bias': _L0_ffn_in['corr_bias'], 'L0_ffn_gate_w': _L0_ffn_in['gate_w'], 'L0_ffn_up_w': _L0_ffn_in['up_w'], 'L0_ffn_down_w': _L0_ffn_in['down_w'], 'L0_ffn_sh_gate_w': _L0_ffn_in['sh_gate_w'], 'L0_ffn_sh_up_w': _L0_ffn_in['sh_up_w'], 'L0_ffn_sh_down_w': _L0_ffn_in['sh_down_w'], 'L0_c': _L0_c, 'L0_wmod': _L0_wmod}
    _x0 = _d['L0_attn_x']
    _d['L0_attn_x'] = jax.random.normal(jax.random.fold_in(jax.random.key(seed), 1), (2, 1024, 256), dtype=_x0.dtype)
    del _x0
    return _d

def reference(L0_attn_x, L0_attn_w_qkv, L0_attn_w_proj, L0_attn_b_proj, L0_ffn_w_router, L0_ffn_corr_bias, L0_ffn_gate_w, L0_ffn_up_w, L0_ffn_down_w, L0_ffn_sh_gate_w, L0_ffn_sh_up_w, L0_ffn_sh_down_w, L0_c, L0_wmod):

    def _L0_attn_ref(x, w_qkv, w_proj, b_proj):
        import jax, jax.numpy as jnp
        import numpy as np
        EPS = 1e-15
        HEAD_DIM = 32
        PAD_VAL = 1.0
        B, N, C = x.shape
        d = HEAD_DIM
        h = C // d
        qkv = (x @ w_qkv.T).reshape(B, N, 3, C)
        q, k, v = (qkv[:, :, 0], qkv[:, :, 1], qkv[:, :, 2])

        def to_heads(t):
            return t.reshape(B, N, h, d).transpose(0, 2, 3, 1)
        q = jax.nn.relu(to_heads(q))
        k = jax.nn.relu(to_heads(k))
        v = to_heads(v)
        v_pad = jnp.pad(v, ((0, 0), (0, 0), (0, 1), (0, 0)), constant_values=PAD_VAL)
        vk = jnp.einsum('bhen,bhdn->bhed', v_pad, k)
        out = jnp.einsum('bhed,bhdn->bhen', vk, q)
        out = out[:, :, :-1] / (out[:, :, -1:] + EPS)
        out = out.reshape(B, C, N).transpose(0, 2, 1)
        return out @ w_proj.T + b_proj

    def _L0_ffn_ref(x, w_router, corr_bias, gate_w, up_w, down_w, sh_gate_w, sh_up_w, sh_down_w):
        import jax, jax.numpy as jnp
        import numpy as np
        H = 256
        M = 176
        E = 32
        TOPK = 6
        G = 8
        TOPK_G = 4
        SH = 2
        B, S = (1, 128)
        b, s, h = x.shape
        xf = x.reshape(-1, h)
        T = xf.shape[0]
        logits = xf @ w_router
        scores = jax.nn.sigmoid(logits)
        sfc = scores + corr_bias
        grp = sfc.reshape(T, G, E // G)
        top2, _ = jax.lax.top_k(grp, 2)
        group_scores = top2.sum(-1)
        _, gidx = jax.lax.top_k(group_scores, TOPK_G)
        group_mask = jax.nn.one_hot(gidx, G, dtype=jnp.float32).sum(axis=1) > 0
        score_mask = jnp.repeat(group_mask, E // G, axis=1)
        masked = jnp.where(score_mask, sfc, -jnp.inf)
        _, topk_idx = jax.lax.top_k(masked, TOPK)
        topk_w = jnp.take_along_axis(scores, topk_idx, axis=1)
        combine = jnp.zeros((T, E), dtype=x.dtype).at[jnp.arange(T)[:, None], topk_idx].add(topk_w)
        g = jnp.einsum('th,ehm->etm', xf, gate_w)
        u = jnp.einsum('th,ehm->etm', xf, up_w)
        eo = jnp.einsum('etm,emh->eth', jax.nn.silu(g) * u, down_w)
        routed = jnp.einsum('te,eth->th', combine, eo)
        shared = jax.nn.silu(xf @ sh_gate_w) * (xf @ sh_up_w) @ sh_down_w
        return (routed + shared).reshape(b, s, h)
    x = L0_attn_x
    mod = (_silu(L0_c) @ L0_wmod).reshape(L0_c.shape[0], 6, 1, -1)
    sa, ca, ga, sb, cb, gb = (mod[:, 0], mod[:, 1], mod[:, 2], mod[:, 3], mod[:, 4], mod[:, 5])
    ga = (2 * (ga >= 0) - 1) * jnp.maximum(jnp.abs(ga), 0.25)
    gb = (2 * (gb >= 0) - 1) * jnp.maximum(jnp.abs(gb), 0.25)
    h = _layernorm(x, axis=-1) * (1 + ca) + sa
    x = x + ga * _L0_attn_ref(h, L0_attn_w_qkv, L0_attn_w_proj, L0_attn_b_proj)
    h = _layernorm(x, axis=-1) * (1 + cb) + sb
    x = x + gb * _L0_ffn_ref(h, L0_ffn_w_router, L0_ffn_corr_bias, L0_ffn_gate_w, L0_ffn_up_w, L0_ffn_down_w, L0_ffn_sh_gate_w, L0_ffn_sh_up_w, L0_ffn_sh_down_w)
    return x

_drawn_inputs = setup_inputs


def setup_inputs(seed=0):
    import zlib

    import numpy as np

    out = dict(_drawn_inputs(seed))
    spreads = {}
    factors = {'L0_attn_w_qkv': 4.927,
     'L0_attn_w_proj': 4.499,
     'L0_attn_b_proj': 8.0,
     'L0_ffn_w_router': 8.0,
     'L0_ffn_corr_bias': 8.0,
     'L0_ffn_gate_w': 8.0,
     'L0_ffn_up_w': 8.0,
     'L0_ffn_down_w': 8.0,
     'L0_ffn_sh_gate_w': 8.0,
     'L0_ffn_sh_up_w': 8.0,
     'L0_ffn_sh_down_w': 8.0,
     'L0_c': 3.778,
     'L0_wmod': 3.798}
    for name, (base, spread) in spreads.items():
        noise = np.random.default_rng([zlib.crc32(name.encode()), seed]).standard_normal(out[name].shape)
        drawn = base * np.exp(spread * noise) if base else spread * noise
        out[name] = jnp.asarray(drawn.astype(out[name].dtype))
    for name, factor in factors.items():
        out[name] = (out[name] * factor).astype(out[name].dtype)
    return out
```

```python
def build_block(nc, x_in, w_qkv, w_proj, b_proj, w_router, corr_bias, gate_w, up_w, down_w,
                sh_gate_w, sh_up_w, sh_down_w, cond, w_mod, out):
    import concourse.bass as bass
    from concourse import mybir
    from contextlib import ExitStack

    f32, i32, u32, bf16 = mybir.dt.float32, mybir.dt.int32, mybir.dt.uint32, mybir.dt.bfloat16
    ALU, ACT, AX = mybir.AluOpType, mybir.ActivationFunctionType, mybir.AxisListType

    P = 128
    B, N, C = x_in.shape
    T = B * N
    NT = T // P
    TB = NT // B
    GT = 4
    NG = TB // GT
    W = GT * P
    KC = C // P
    HD = 32
    NH = C // HD
    HH = NH // KC
    VE = HD + 1
    E, _, M = gate_w.shape
    M2 = 2 * M
    KD = M // 2
    SM = sh_gate_w.shape[1]
    SC = [(a, min(P, SM - a)) for a in range(0, SM, P)]
    TOPK, G, TOPG = 6, 8, 4
    EG = E // G
    NBLK = (T * TOPK - E) // P + E + 1
    TURNS = -(-NBLK // 4)
    FEWEST = T * TOPK // P // 4 - 1
    MAP_W = P + 8
    NCOL = E * NT + 1
    EMPTY = NCOL - 1
    LN_EPS, DIV_EPS, GUARD = 1e-5, 1e-15, 0.25
    LOW = -3.0e38

    x_v = x_in.rearrange("b (i p) c -> p (b i) c", p=P)
    out_v = out.rearrange("b (i p) c -> p (b i) c", p=P)

    ctx = ExitStack()
    with ctx:
        def sb(name, shape, dt=f32):
            return ctx.enter_context(nc.sbuf_tensor(name, shape, dt))

        def sem(name):
            return ctx.enter_context(nc.semaphore(name))

        def shared_part(region, width):
            at = [0]

            def take(n):
                a = at[0]
                at[0] += n
                assert at[0] <= width, (at[0], width)
                return region[:, a:a + n]
            return take

        h2_dram = nc.dram_tensor("h2_rows", (T, C), f32).ap()
        lists = nc.dram_tensor("pair_lists", (P * NCOL, 4), f32).ap()
        pair_rows = nc.dram_tensor("pair_rows", (T * TOPK, C), f32).ap()
        h2_tiles = h2_dram.rearrange("(i p) c -> p i c", p=P)
        lists_v = lists.rearrange("(p n) w -> p (n w)", p=P)
        pairs_v = pair_rows.rearrange("(i p k) c -> p i (k c)", p=P, k=TOPK)

        EARLY = 24
        gate_up = sb("gate_up", [P, E * KC * M2])
        gu_v = gate_up[:, :].rearrange("p (e k m) -> p e k m", e=E, k=KC)
        down = sb("down", [P, 2 * E * C])
        dn_v = down[:, :].rearrange("p (m f) -> p m f", m=2)
        X = sb("X", [P, NT, C])
        tok_buf = sb("tok_buf", [P, NT * C])
        xn = tok_buf[:, :].rearrange("p (i c) -> p i c", i=NT)
        h2T = tok_buf[:, :].rearrange("p (b k n) -> p b k n", b=B, k=KC)
        sh_gu = sb("sh_gu", [P, 2, KC, SM])
        sh_dn = sb("sh_dn", [P, len(SC), C])
        router = sb("router", [P, KC, E])
        bias_bc = sb("bias_bc", [P, E])
        gb = sb("gb", [P, B, C])
        lists_sb = sb("lists_sb", [P, NCOL * 4])
        sT = lists_sb[:, 0:len(SC) * W].rearrange("p (m n) -> p m n", m=len(SC))
        sh_tmp = lists_sb[:, len(SC) * W:len(SC) * W + C]
        recs = sb("recs", [P, NT, TOPK, 4])
        rows_i = sb("rows_i", [P, NT, TOPK], i32)
        ident = sb("ident", [P, P])
        tri = sb("tri", [P, P], bf16)
        ones_bf = sb("ones_bf", [P, P], bf16)
        iota_e = sb("iota_e", [P, E])
        iota_p = sb("iota_p", [P, 1])
        used = sb("used", [P, E])
        stats = sb("stats", [P, NT, 6])
        mv = sb("mv", [P, NT, 2])
        mv2 = sb("mv2", [P, NT, 2])
        rstd = sb("rstd", [P, NT])
        rstd2 = sb("rstd2", [P, NT])
        half = sb("half", [P, TB])
        modT = sb("modT", [P, 4, B])
        mapf = sb("mapf", [P, 4])
        iota_n = sb("iota_n", [P, NT])

        part = shared_part(down, 2 * E * C)
        wmod_sb = part(KC * 6 * C).rearrange("p (k n) -> p k n", k=KC)
        route_tmp = wmod_sb
        c_row = part(C)[0:B, :]
        csT = part(KC * B).rearrange("p (k b) -> p k b", k=KC)
        csB = part(KC * B * P).rearrange("p (k b n) -> p k b n", k=KC, b=B)
        wqkv_raw = part(3 * KC * C).rearrange("p (o c) -> p o c", o=3 * KC)
        wproj_raw = part(KC * C).rearrange("p (o c) -> p o c", o=KC)
        wT = part(KC * 3 * C).rearrange("p (k o) -> p k o", k=KC)
        wpT = part(B * KC * C).rearrange("p (b k o) -> p b k o", b=B, k=KC)
        rows = part(B * 4 * C).rearrange("p (b r c) -> p b r c", b=B, r=4)
        bga = part(B * C).rearrange("p (b c) -> p b c", b=B)
        hT = part(KC * N // 2).rearrange("p (k n) -> p k n", k=KC)
        qT = part(KC * N).rearrange("p (k n) -> p k n", k=KC)
        kk = part(2 * C).rearrange("p (s c) -> p s c", s=2)
        vv = part(2 * NH * VE).rearrange("p (s h e) -> p s h e", s=2, h=NH)
        nd = part(KC * 2 * P).rearrange("p (k a n) -> p k a n", k=KC, a=2)
        rden = part(W)
        oT = wqkv_raw[:, 0:KC * W // C, :].rearrange("p o c -> p (o c)").rearrange("p (k n) -> p k n", k=KC)

        part = shared_part(gate_up[:, EARLY * KC * M2:], (E - EARLY) * KC * M2)
        h2 = part(TB * C).rearrange("p (i c) -> p i c", i=TB)
        chosen = part(TB * TOPK * E).rearrange("p (i k e) -> p i k e", i=TB, k=TOPK)
        score = part(TB * E).rearrange("p (i e) -> p i e", i=TB)
        sfc = part(TB * E).rearrange("p (i e) -> p i e", i=TB)
        sel = part(TB * E).rearrange("p (i e) -> p i e", i=TB)
        sel_bf = part(TB * E // 2).bitcast(bf16).rearrange("p (i e) -> p i e", i=TB)
        rank = part(TB * E).rearrange("p (i e) -> p i e", i=TB)
        tmp = wmod_sb[:, :, :].rearrange("p k n -> p (k n)")
        weighed = tmp[:, 0:TB * TOPK * E].rearrange("p (i k e) -> p i k e", i=TB, k=TOPK)
        at = TB * TOPK * E
        rank_i = tmp[:, at:at + 2 * TB * E].bitcast(i32).rearrange("p (a i e) -> p a i e", a=2, i=TB)
        at += 2 * TB * E
        pair = tmp[:, at:at + 4 * TB * G].rearrange("p (a i g) -> p a i g", a=4, i=TB)
        at += 4 * TB * G
        gs = tmp[:, at:at + TB * G].rearrange("p (i g) -> p i g", i=TB)
        at += TB * G
        gmask = tmp[:, at:at + 2 * TB * G].rearrange("p (a i g) -> p a i g", a=2, i=TB)
        at += 2 * TB * G
        top = tmp[:, at:at + TB * 8].rearrange("p (i k) -> p i k", i=TB)
        at += TB * 8
        top_f = tmp[:, at:at + TB * 8].rearrange("p (i k) -> p i k", i=TB)
        at += TB * 8
        top_i = tmp[:, at:at + TB * 8].bitcast(u32).rearrange("p (i k) -> p i k", i=TB)
        at += TB * 8
        assert at <= KC * 6 * C

        part = shared_part(tok_buf, NT * C // 2)
        R = 4
        xg = part(R * C).rearrange("p (s c) -> p s c", s=R)
        xT = part(2 * C).rearrange("p (s k n) -> p s k n", s=2, k=KC)
        aT = part(2 * 2 * P).rearrange("p (s m n) -> p s m n", s=2, m=2)
        part = shared_part(tok_buf[:, NT * C // 2:], NT * C // 2)
        yw = part(R * C).rearrange("p (s c) -> p s c", s=R)
        act_g = part(2 * M).rearrange("p (s m) -> p s m", s=2)
        act = part(2 * M).rearrange("p (s m) -> p s m", s=2)
        map_i = part(2 * MAP_W + 1)[0:1, :].bitcast(i32)
        more = yw.rearrange("p s c -> p (s c)")[:, 0:E * NT].rearrange("p (e n) -> p e n", e=E)
        seg = yw.rearrange("p s c -> p (s c)")[:, E * NT:(NT + 4) * E].rearrange("p (a e) -> p a e", a=4)
        tok_i = sb("tok_i", [P, R], i32)
        dest_i = sb("dest_i", [P, R], i32)
        pair_w = sb("pair_w", [P, R])
        part = shared_part(gate_up, E * KC * M2)
        ring = [part(TOPK * C).rearrange("p (k c) -> p k c", k=TOPK) for _ in range(4)]
        sums = [part(3 * C).rearrange("p (k c) -> p k c", k=3) for _ in range(2)]
        prod = [part(C) for _ in range(2)]

        banks = [ctx.enter_context(nc.psum_tensor(f"bank{i}", [P, 512], f32)) for i in range(8)]

        filled = [sem(f"bank{i}_filled") for i in range(8)]
        drained = [sem(f"bank{i}_drained") for i in range(8)]
        ld_c, ld_mod, ld_qkv, ld_proj, ld_route, ld_sh = (sem("ld_" + n) for n in ("c", "mod", "qkv", "proj", "route", "shared"))
        ld_x = [sem(f"ld_x{i}") for i in range(NT // GT)]
        ld_early, ld_late, ld_lists = sem("ld_early_weights"), sem("ld_late_weights"), sem("ld_lists")
        consts = sem("constants_ready")
        pool_passed = sem("pool_passed_waits")
        dve_own, pool_own = sem("dve_own_steps"), sem("pool_own_steps")
        var_ready, rstd_ready, xn_ready, xb_ready = (sem(n) for n in ("var_ready", "rstd_ready", "xn_ready", "xb_ready"))
        cs_ready, wpT_ready, kv_used = (
            sem(n) for n in ("csB_ready", "gated_projection_ready", "keys_values_used"))
        var2_ready, rstd2_ready, xn2_ready, h2_ready, h2_stored = (
            sem(n) for n in ("var2_ready", "rstd2_ready", "xn2_ready", "h2_ready", "h2_stored"))
        sel_ready, recs_ready, lists_clear, listed = (
            sem(n) for n in ("chosen_ready", "records_ready", "lists_clear", "listed"))
        mapf_ready = sem("map_columns_ready")
        tok_listed, dest_listed = sem("block_tokens_ready"), sem("block_dests_ready")
        gathered = [sem(f"gathered{s}") for s in range(R)]
        scattered = [sem(f"scattered{s}") for s in range(R)]
        x_turned, xT_copied, gu_done, silu_done, act_done, act_turned, aT_copied, y_done, y_scaled = (
            sem(n) for n in ("x_turned", "xT_copied", "gate_up_done", "silu_done", "act_done", "act_turned", "aT_copied", "y_done", "y_scaled"))
        fetched = [sem(f"rows_fetched{s}") for s in range(4)]
        summed, out_ready, stored = sem("rows_summed"), sem("out_ready"), sem("out_stored")

        use = {}
        uses = [0] * 8

        def plan(key, bank):
            uses[bank] += 1
            use[key] = bank, uses[bank]

        plan(("c",), 7)
        for b in range(B):
            for s in range(2):
                plan(("mod", b, s), (2 * b + s) % 2)
        plan(("modT",), 2)
        for g in range(2 * KC):
            plan(("wT", g), 3 + g % 2)
        for k in range(KC):
            plan(("wpT", k), 5 + k)

        def plan_keys_values(b):
            for g in range(NG):
                for k in range(KC):
                    plan(("hT", b, g, k), k)
                for k in range(KC):
                    plan(("q", b, g, k), 2 + k)
                for i in range(GT):
                    plan(("kv", b, g * GT + i), 4 + i % 2)
            for k in range(KC):
                plan(("vk", b, k), 6 + k)

        def plan_attend(b):
            for g in range(NG):
                for k in range(KC):
                    plan(("num", b, g, k), 2)
                    plan(("den", b, g, k), 3)
                for i in range(GT):
                    plan(("proj", b, g * GT + i), 4 + i % 2)

        def plan_turn(b):
            for g in range(NG):
                for k in range(KC):
                    plan(("h2T", b, g, k), k)
            plan(("router", b), 2)

        def plan_ranks(b):
            plan(("ranks", b), 3)

        def plan_shared(b):
            for g in range(NG):
                for m in range(len(SC)):
                    plan(("sg", b, g, m), 2 * (m % 2))
                    plan(("su", b, g, m), 2 * (m % 2) + 1)
                for i in range(GT):
                    plan(("sd", b, g * GT + i), 4 + i % 2)

        plan_keys_values(0)
        plan_attend(0)
        plan_turn(0)
        plan_keys_values(1)
        plan_ranks(0)
        plan_attend(1)
        plan_turn(1)
        plan_shared(0)
        plan_ranks(1)
        plan_shared(1)
        plan(("map",), 6)

        def of(key):
            return banks[use[key][0]]

        def fill(pe, key):
            bank, n = use[key]
            if n > 1:
                pe.wait_ge(drained[bank], n - 1)
            return banks[bank]

        def await_result(eng, key):
            bank, n = use[key]
            eng.wait_ge(filled[bank], n)
            return banks[bank]

        def full(key):
            return filled[use[key][0]]

        def free(key):
            return drained[use[key][0]]

        def await_computed(eng, key):
            eng.wait_ge(full(key), use[key][1])

        def await_read(eng, key):
            eng.wait_ge(free(key), use[key][1])

        def wait(eng, s, value):
            if not isinstance(value, int) or value > 0:
                eng.wait_ge(s, value)

        def load_last_turn(eng):
            return 1 + eng.value_load(map_i[0:1, 2 * MAP_W:2 * MAP_W + 1], min_val=FEWEST - 1, max_val=TURNS - 2)

        def load_values(eng, which, section, turn):
            _, values = nc.values_load_multi_w_load_instructions(
                map_i[0:1, bass.ds(section * MAP_W + R * turn, 2 * R)], engines=(which,),
                skip_runtime_bounds_check_because="the map's entries are clamped where they are made")
            return values

        def blocks(eng, step):
            last_turn = load_last_turn(eng)
            step(0, False)
            with eng.Fori(1, TURNS - 1) as turn:
                with eng.If(turn < last_turn):
                    step(turn, False)
            step(last_turn, True)

        block = ctx.enter_context(nc.Block())

        @block.sync
        def _(sp):
            sp.dma_start(c_row, cond).then_inc(ld_c, 16)
            sp.dma_start(wmod_sb, w_mod.rearrange("(k p) n -> p k n", p=P)).then_inc(ld_mod, 16)
            sp.dma_start(X[:, 0:GT, :], x_v[:, 0:GT, :]).then_inc(ld_x[0], 16)
            sp.dma_start(wqkv_raw, w_qkv.rearrange("(o p) c -> p o c", p=P)).then_inc(ld_qkv, 16)
            sp.dma_start(wproj_raw, w_proj.rearrange("(o p) c -> p o c", p=P)).then_inc(ld_proj, 16)
            sp.dma_start(bga[:, 0, :], b_proj.partition_broadcast(P)).then_inc(ld_proj, 16)
            for g in range(1, NT // GT):
                sp.dma_start(X[:, g * GT:(g + 1) * GT, :], x_v[:, g * GT:(g + 1) * GT, :]).then_inc(ld_x[g], 16)
            sp.dma_start(router[:, :, :], w_router.rearrange("(k p) e -> p k e", p=P)).then_inc(ld_route, 16)
            sp.dma_start(bias_bc[:, :], corr_bias.partition_broadcast(P)).then_inc(ld_route, 16)
            for a, w in enumerate((sh_gate_w, sh_up_w)):
                sp.dma_start(sh_gu[:, a, :, :], w.rearrange("(k p) m -> p k m", p=P)).then_inc(ld_sh, 16)
            for m, (a, n) in enumerate(SC):
                sp.dma_start(sh_dn[0:n, m, :], sh_down_w[a:a + n, :]).then_inc(ld_sh, 16)
            sp.wait_ge(consts, 7)
            sp.dma_start(lists_v, lists_sb[:, :]).then_inc(lists_clear, 16)

            def load_gate_up(e0, e1, s):
                for a, w in enumerate((gate_w, up_w)):
                    for k in range(KC):
                        sp.dma_start(gu_v[:, e0:e1, k, a * M:(a + 1) * M],
                                     w[e0:e1, k * P:(k + 1) * P, :].rearrange("e p m -> p e m")).then_inc(s, 16)

            for e in range(0, EARLY, 8):
                load_gate_up(e, e + 8, ld_early)
            for b in range(B):
                for g in range(NG):
                    sp.wait_ge(h2_ready, b * TB + (g + 1) * GT)
                    t = b * TB + g * GT
                    sp.dma_start(h2_tiles[:, t:t + GT, :], h2[:, g * GT:(g + 1) * GT, :]).then_inc(h2_stored, 16)
            sp.wait_ge(h2_stored, 16 * B * NG)
            await_computed(sp, ("h2T", B - 1, NG - 1, KC - 1))
            sp.wait_ge(recs_ready, B)
            for m in range(2):
                sp.dma_start(dn_v[0:KD, m, :].rearrange("p (e c) -> p e c", e=E),
                             down_w[:, m * KD:(m + 1) * KD, :].rearrange("e p c -> p e c")).then_inc(ld_late, 16)
            load_gate_up(EARLY, E, ld_late)
            sp.wait_ge(listed, 16 * NT * TOPK)
            sp.wait_ge(mapf_ready, 1)
            sp.dma_start(lists_sb[:, :], lists_v).then_inc(ld_lists, 16)
            await_read(sp, ("map",))
            last_turn = load_last_turn(sp)
            for s in range(R):
                sp.wait_ge(scattered[s], 16 * last_turn + 16)
            for t in range(NT):
                if t >= 4:
                    sp.wait_ge(summed, t - 3)
                sp.dma_start(ring[t % 4].rearrange("p k c -> p (k c)"), pairs_v[:, t, :]).then_inc(fetched[t % 4], 16)
                if t % 4 == 3 and t > 4:
                    sp.wait_ge(out_ready, t - 3)
                    sp.dma_start(out_v[:, t - 7:t - 3, :], X[:, t - 7:t - 3, :]).then_inc(stored, 16)
            sp.wait_ge(out_ready, NT)
            sp.dma_start(out_v[:, NT - 4:NT, :], X[:, NT - 4:NT, :]).then_inc(stored, 16)
            sp.wait_ge(stored, 16 * NT // 4)

        @block.gpsimd
        def _(pool):
            done = [0]

            def link(ins):
                done[0] += 1
                ins.then_inc(pool_own, 1)
                pool.wait_ge(pool_own, done[0])

            link(nc.gpsimd.memset(ident[:, :], 0.0))
            nc.gpsimd.affine_select(out=ident[:, :], in_=ident[:, :], compare_op=ALU.not_equal, fill=1.0,
                                    base=0, pattern=[[-1, P]], channel_multiplier=1).then_inc(consts, 1)
            nc.gpsimd.memset(half[:, :], -0.5).then_inc(consts, 1)
            link(nc.gpsimd.memset(ones_bf[:, :], 1.0))
            nc.gpsimd.affine_select(out=tri[:, :], in_=ones_bf[:, :], compare_op=ALU.is_gt, fill=0.0,
                                    base=0, pattern=[[1, P]], channel_multiplier=-1).then_inc(consts, 1)
            nc.gpsimd.iota(iota_e[:, :], [[1, E]], base=0, channel_multiplier=0,
                           allow_small_or_imprecise_dtypes=True).then_inc(consts, 1)
            nc.gpsimd.iota(iota_p[:, :], [[1, 1]], base=0, channel_multiplier=1,
                           allow_small_or_imprecise_dtypes=True).then_inc(consts, 1)
            nc.gpsimd.memset(vv[:, :, :, HD:VE], 1.0).then_inc(consts, 1)
            link(nc.gpsimd.memset(lists_sb[:, :], 0.0))
            nc.gpsimd.iota(lists_sb[:, :].rearrange("p (n w) -> p n w", w=4)[:, :, 1:2], [[0, NCOL]],
                           base=T * TOPK, channel_multiplier=1,
                           allow_small_or_imprecise_dtypes=True).then_inc(consts, 1)
            link(nc.gpsimd.memset(recs[:, :, :, :], 0.0))
            nc.gpsimd.iota(recs[:, :, :, 0], [[P, NT], [0, TOPK]], base=0, channel_multiplier=1,
                           allow_small_or_imprecise_dtypes=True)
            nc.gpsimd.iota(recs[:, :, :, 1], [[P * TOPK, NT], [1, TOPK]], base=0, channel_multiplier=TOPK,
                           allow_small_or_imprecise_dtypes=True).then_inc(consts, 1)
            nc.gpsimd.memset(used[:, :], 0.0)
            nc.gpsimd.iota(iota_n[:, :], [[P, NT]], base=0, channel_multiplier=0,
                           allow_small_or_imprecise_dtypes=True).then_inc(consts, 1)
            nc.gpsimd.memset(nd, 0.0).then_inc(consts, 1)

            def power(out_ap, var_ap, n):
                link(nc.gpsimd.tensor_scalar(out_ap, var_ap, LN_EPS, None, ALU.add))
                return nc.gpsimd.tensor_tensor(out_ap, out_ap, half[:, 0:n], ALU.pow)

            pool.wait_ge(consts, 10)
            for g in range(NT // GT):
                a, z = g * GT, (g + 1) * GT
                pool.wait_ge(var_ready, z)
                power(rstd[:, a:z], mv[:, a:z, 1], GT).then_inc(rstd_ready, 1)
            pool.wait_ge(wpT_ready, 1)
            for t in range(NT):
                pool.wait_ge(xn_ready, t + 1)
                nc.gpsimd.tensor_tensor(X[:, t, :], X[:, t, :], bga[:, t // TB, :], ALU.add).then_inc(xb_ready, 1)

            def second_norm(b):
                for g in range(NG):
                    a = b * TB + g * GT
                    pool.wait_ge(var2_ready, a + GT)
                    power(rstd2[:, a:a + GT], mv2[:, a:a + GT, 1], GT).then_inc(rstd2_ready, 1)
                    for i in range(g * GT, (g + 1) * GT):
                        pool.wait_ge(xn2_ready, b * TB + i + 1)
                        link(nc.gpsimd.tensor_tensor(h2[:, i, :], h2[:, i, :], rows[:, b, 2, :], ALU.mult))
                        nc.gpsimd.tensor_tensor(h2[:, i, :], h2[:, i, :], rows[:, b, 1, :], ALU.add).then_inc(h2_ready, 1)

            def list_pairs(a, z):
                pool.wait_ge(recs_ready, a // TB + 1)
                if a == 0:
                    pool.wait_ge(lists_clear, 16)
                for t in range(a, z):
                    for k in range(TOPK):
                        nc.gpsimd.indirect_dma_start(
                            out=lists, out_offset=bass.IndirectOffsetOnAxis(ap=rows_i[:, t, k:k + 1], axis=0),
                            in_=recs[:, t, k, :], in_offset=None).then_inc(listed, 16)

            second_norm(0)
            list_pairs(0, TB // 2)
            second_norm(1)
            list_pairs(TB // 2, TB)
            list_pairs(TB, NT)

            pool.wait_ge(h2_stored, 16 * B * NG)
            await_computed(pool, ("sd", 0, TB - 1))

            await_read(pool, ("map",))

            def fetch(s):
                nc.gpsimd.indirect_dma_start(
                    out=xg[:, s, :], out_offset=None, in_=h2_dram,
                    in_offset=bass.IndirectOffsetOnAxis(ap=tok_i[:, s:s + 1], axis=0)).then_inc(gathered[s], 16)

            for s in range(R):
                pool.wait_ge(tok_listed, s + 1)
                fetch(s)

            def gather_next(c, turn):
                pool.wait_ge(tok_listed, R * turn + R + c + 1)
                pool.wait_ge(x_turned, R * turn + c + 1)
                pool.sem_inc(pool_passed, 1)
                fetch(c)

            def scatter(c, turn):
                pool.wait_ge(y_scaled, R * turn + c + 1)
                pool.sem_inc(pool_passed, 1)
                nc.gpsimd.indirect_dma_start(
                    out=pair_rows, out_offset=bass.IndirectOffsetOnAxis(ap=dest_i[:, c:c + 1], axis=0),
                    in_=yw[:, c, :], in_offset=None, bounds_check=T * TOPK - 1,
                    oob_is_err=False).then_inc(scattered[c], 16)

            def step(turn, last):
                for c in range(R):
                    if not last:
                        gather_next(c, turn)
                    scatter(c, turn)

            blocks(pool, step)
            for t in range(NT):
                pool.wait_ge(summed, t + 1)
                link(nc.gpsimd.tensor_tensor(prod[t % 2], sums[t % 2][:, 0, :], gb[:, t // TB, :], ALU.mult))
                nc.gpsimd.tensor_tensor(X[:, t, :], X[:, t, :], prod[t % 2], ALU.add).then_inc(out_ready, 1)

        @block.scalar
        def _(act_e):
            ps = await_result(act_e, ("c",))
            nc.scalar.activation(csT, ps[:, 0:KC * B].rearrange("p (k b) -> p k b", k=KC),
                                 ACT.Silu).then_inc(free(("c",)), 1)

            def keys_values(b):
                for g in range(NG):
                    n = b * NG + g
                    for k in range(KC):
                        ps = await_result(act_e, ("hT", b, g, k))
                        if n == 0 and k == 0:
                            await_read(act_e, ("modT",))
                        nc.scalar.activation(hT[:, k, :], ps[:, :], ACT.Identity, bias=modT[:, k, b:b + 1],
                                             scale=modT[:, KC + k, b:b + 1]).then_inc(free(("hT", b, g, k)), 1)
                    if b >= 1 and g == 0:
                        await_computed(act_e, ("den", b - 1, NG - 1, KC - 1))
                    for k in range(KC):
                        ps = await_result(act_e, ("q", b, g, k))
                        nc.scalar.activation(qT[:, k, g * W:(g + 1) * W], ps[:, :], ACT.Relu).then_inc(free(("q", b, g, k)), 1)
                    for i in range(GT):
                        t = b * TB + g * GT + i
                        key = ("kv", b, g * GT + i)
                        ps = await_result(act_e, key)
                        if t >= 2:
                            if (t - 2) % TB == TB - 1:
                                await_computed(act_e, ("vk", (t - 2) // TB, KC - 1))
                            else:
                                act_e.wait_ge(kv_used, t - 1 - (t - 2) // TB)
                        if t == 0:
                            act_e.wait_ge(consts, 10)
                        nc.scalar.activation(kk[:, t % 2, :], ps[:, 0:C], ACT.Relu)
                        nc.scalar.activation(vv[:, t % 2, :, 0:HD], ps[:, C:2 * C].rearrange("p (h e) -> p h e", h=NH),
                                             ACT.Copy).then_inc(free(key), 1)

            def turned(b):
                for g in range(NG):
                    for k in range(KC):
                        key = ("h2T", b, g, k)
                        ps = await_result(act_e, key)
                        nc.scalar.activation(h2T[:, b, k, g * W:(g + 1) * W], ps[:, :], ACT.Copy).then_inc(free(key), 1)
                key = ("router", b)
                ps = await_result(act_e, key)
                if b == 1:
                    act_e.wait_ge(recs_ready, 1)
                nc.scalar.activation(score, ps[:, 0:TB * E].rearrange("p (i e) -> p i e", i=TB),
                                     ACT.Sigmoid).then_inc(free(key), 1)

            def shared(b):
                for g in range(NG):
                    for m, (a, n) in enumerate(SC):
                        key = ("sg", b, g, m)
                        ps = await_result(act_e, key)
                        if (b, g) != (0, 0) and m == 0:
                            await_computed(act_e, ("sd", b, g * GT - 1) if g else ("sd", b - 1, TB - 1))
                        if (b, g, m) == (0, 0, 0):
                            act_e.wait_ge(lists_clear, 16)
                        nc.scalar.activation(sT[0:n, m, :], ps[0:n, :], ACT.Silu).then_inc(free(key), 1)

            keys_values(0)
            turned(0)
            keys_values(1)
            turned(1)
            shared(0)
            shared(1)

            def silu(c, n):
                act_e.wait_ge(gu_done, n + 1)
                if not isinstance(n, int) or n >= 2:
                    act_e.wait_ge(act_done, n - 1)
                nc.scalar.activation(act_g[:, c % 2, :], banks[1 + c % 2][:, 0:M], ACT.Silu).then_inc(silu_done, 1)

            await_read(act_e, ("map",))
            silu(0, 0)

            def step(turn, last):
                for c in range(R):
                    block_step(c, turn, last and c == R - 1)

            def block_step(c, turn, last):
                n = R * turn + c
                act_e.wait_ge(act_turned, n + 1)
                if not isinstance(n, int) or n >= 2:
                    act_e.wait_ge(y_done, n - 1)
                nc.scalar.activation(aT[0:KD, c % 2, :, :], banks[3][0:KD, 0:2 * P].rearrange("p (m n) -> p m n", m=2),
                                     ACT.Copy).then_inc(aT_copied, 1)
                if not last:
                    silu(c + 1, n + 1)
                act_e.wait_ge(y_done, n + 1)
                act_e.wait_ge(dest_listed, n + 1)
                if not isinstance(turn, int) or turn > 0:
                    act_e.wait_ge(scattered[c], 16 * turn)
                nc.scalar.activation(yw[:, c, :], banks[4 + c % 2][:, 0:C], ACT.Copy,
                                     scale=pair_w[:, c:c + 1]).then_inc(y_scaled, 1)

            blocks(act_e, step)

        @block.vector
        def _(dve):
            done = [0]

            def link(ins):
                done[0] += 1
                ins.then_inc(dve_own, 1)
                dve.wait_ge(dve_own, done[0])

            def link_free(ins, key):
                ins.then_inc(free(key), 1)
                await_read(dve, key)

            V = nc.vector
            await_read(dve, ("c",))
            V.tensor_copy(csB, csT.unsqueeze(3).broadcast_to([P, KC, B, P])).then_inc(cs_ready, 1)

            def first_norm(g):
                dve.wait_ge(ld_x[g], 16)
                for t in range(g * GT, (g + 1) * GT):
                    link(V.bn_stats(stats[:, t, :], X[:, t, :]))
                    V.bn_aggr(mv[:, t, :], stats[:, t, :]).then_inc(var_ready, 1)

            def normalise(g):
                dve.wait_ge(rstd_ready, g + 1)
                dve.wait_ge(var_ready, (g + 1) * GT)
                for t in range(g * GT, (g + 1) * GT):
                    V.tensor_scalar(xn[:, t, :], X[:, t, :], mv[:, t, 0:1], rstd[:, t:t + 1],
                                    ALU.subtract, ALU.mult).then_inc(xn_ready, 1)

            first_norm(0)
            
            for b in range(B):
                for s in range(2):
                    key = ("mod", b, s)
                    ps = await_result(dve, key)
                    gate = rows[:, b, 0, :] if s == 0 else gb[:, b, :]
                    src = ps[:, 0:C] if s == 0 else ps[:, C:2 * C]
                    other = ps[:, C:2 * C] if s == 0 else ps[:, 0:C]
                    link(V.tensor_scalar(rows[:, b, 3, :], src, -1.0, GUARD, ALU.mult, ALU.max))
                    link(V.tensor_tensor(rows[:, b, 3, :], src, rows[:, b, 3, :], ALU.max))
                    link(V.tensor_scalar(gate, src, 0.0, 2.0, ALU.is_ge, ALU.mult))
                    V.tensor_scalar(rows[:, b, 1 + s, :], other, float(s), None, ALU.add).then_inc(free(key), 1)
                    link(V.scalar_tensor_tensor(out=gate, in0=gate, scalar=-1.0, in1=rows[:, b, 3, :],
                                                op0=ALU.add, op1=ALU.mult))
            ps = await_result(dve, ("modT",))
            link(V.tensor_copy(modT[:, 0:KC, :], ps[:, 0:KC * B].rearrange("p (k b) -> p k b", k=KC)))
            V.tensor_scalar(modT[:, KC:2 * KC, :], ps[:, KC * B:2 * KC * B].rearrange("p (k b) -> p k b", k=KC),
                            1.0, None, ALU.add).then_inc(free(("modT",)), 1)
            normalise(0)
            for g in range(2 * KC):
                key = ("wT", g)
                ps = await_result(dve, key)
                n = 3 * C // 2
                V.tensor_copy(wT[:, g // 2, (g % 2) * n:(g % 2 + 1) * n], ps[:, 0:n]).then_inc(free(key), 1)
            for g in range(1, NT // GT):
                first_norm(g)
            for k in range(KC):
                key = ("wpT", k)
                ps = await_result(dve, key)
                for b in range(B):
                    last = V.tensor_tensor(wpT[:, b, k, :], ps[:, 0:C], rows[:, b, 0, :], ALU.mult)
                last.then_inc(free(key), 1)
            dve.wait_ge(ld_proj, 32)
            link(V.tensor_tensor(bga[:, 1, :], bga[:, 0, :], rows[:, 1, 0, :], ALU.mult))
            V.tensor_tensor(bga[:, 0, :], bga[:, 0, :], rows[:, 0, 0, :], ALU.mult).then_inc(wpT_ready, 1)
            for g in range(1, NT // GT):
                normalise(g)

            def attend(b):
                for k in range(KC):
                    key = ("vk", b, k)
                    ps = await_result(dve, key)
                    if k == 0:
                        if b == 0:
                            dve.wait_ge(consts, 10)
                        else:
                            await_computed(dve, ("den", b - 1, NG - 1, KC - 1))
                    for h in range(HH):
                        r = slice(h * HD, (h + 1) * HD)
                        V.tensor_copy(nd[r, k, 0, r], ps[r, h * VE:h * VE + HD])
                        last = V.tensor_copy(nd[r, k, 1, r], ps[r, h * VE + HD:(h + 1) * VE].broadcast_to([HD, HD]))
                    last.then_inc(free(key), 1)
                for g in range(NG):
                    for k in range(KC):
                        ps = await_result(dve, ("den", b, g, k))
                        link_free(V.tensor_scalar(rden, ps[:, :], DIV_EPS, None, ALU.add), ("den", b, g, k))
                        link(V.reciprocal(rden, rden))
                        ps = await_result(dve, ("num", b, g, k))
                        link_free(V.tensor_tensor(oT[:, k, :], ps[:, :], rden, ALU.mult), ("num", b, g, k))
                    for i in range(g * GT, (g + 1) * GT):
                        t = b * TB + i
                        key = ("proj", b, i)
                        ps = await_result(dve, key)
                        dve.wait_ge(xb_ready, t + 1)
                        link_free(V.tensor_tensor(X[:, t, :], ps[:, 0:C], X[:, t, :], ALU.add), key)
                        link(V.bn_stats(stats[:, t, :], X[:, t, :]))
                        V.bn_aggr(mv2[:, t, :], stats[:, t, :]).then_inc(var2_ready, 1)
                    dve.wait_ge(rstd2_ready, b * NG + g + 1)
                    dve.wait_ge(var2_ready, b * TB + (g + 1) * GT)
                    if b == 1 and g == 0:
                        dve.wait_ge(h2_stored, 16 * NG)
                        await_computed(dve, ("h2T", 0, NG - 1, KC - 1))
                    for i in range(g * GT, (g + 1) * GT):
                        t = b * TB + i
                        V.tensor_scalar(h2[:, i, :], X[:, t, :], mv2[:, t, 0:1], rstd2[:, t:t + 1],
                                        ALU.subtract, ALU.mult).then_inc(xn2_ready, 1)

            def over(ap, shape, axis):
                return ap.unsqueeze(axis).broadcast_to(shape)

            def choose(b):
                shape = [P, TB, E]
                key = ("router", b)
                await_read(dve, key)
                if b == 0:
                    dve.wait_ge(ld_route, 32)
                link(V.tensor_tensor(sfc, score, over(bias_bc[:, :], shape, 1), ALU.add))
                q = sfc.rearrange("p i (g j) -> p (i g) j", j=EG)
                flat = [pair[:, a].rearrange("p i g -> p (i g)") for a in range(4)]
                link(V.tensor_tensor(flat[0], q[:, :, 0], q[:, :, 1], ALU.max))
                link(V.tensor_tensor(flat[1], q[:, :, 0], q[:, :, 1], ALU.min))
                link(V.tensor_tensor(flat[2], q[:, :, 2], q[:, :, 3], ALU.max))
                link(V.tensor_tensor(flat[3], q[:, :, 2], q[:, :, 3], ALU.min))
                g_flat = gs.rearrange("p i g -> p (i g)")
                link(V.tensor_tensor(g_flat, flat[0], flat[2], ALU.add))
                link(V.tensor_tensor(flat[1], flat[0], flat[1], ALU.add))
                link(V.tensor_tensor(flat[3], flat[2], flat[3], ALU.add))
                link(V.tensor_tensor(flat[1], flat[1], flat[3], ALU.max))
                link(V.tensor_tensor(g_flat, g_flat, flat[1], ALU.max))

                def largest(values, n, width):
                    for i in range(TB):
                        last = V.max(top[:, i, :], values[:, i, :])
                    link(last)
                    for i in range(TB):
                        last = V.max_index(top_i[:, i, :], top[:, i, :], values[:, i, :])
                    link(last)
                    link(V.tensor_copy(top_f, top_i[:, :, :]))
                    one = chosen[:, :, 0:n, 0:width]
                    s4 = [P, TB, n, width]
                    link(V.tensor_tensor(one, iota_e[:, 0:width].unsqueeze(1).unsqueeze(1).broadcast_to(s4),
                                         top_f[:, :, 0:n].unsqueeze(3).broadcast_to(s4), ALU.is_equal))
                    return one

                if b == 0:
                    dve.wait_ge(consts, 10)
                one = largest(gs, TOPG, G)
                link(V.tensor_reduce(gmask[:, 0], one.rearrange("p i k g -> p i g k"), AX.X, ALU.add))
                link(V.tensor_scalar(gmask[:, 1], gmask[:, 0], -1.0, -LOW, ALU.add, ALU.mult))
                m_q = sel.rearrange("p i (g j) -> p (i g) j", j=EG)
                s3 = [P, TB * G, EG]
                link(V.tensor_tensor(m_q, q, gmask[:, 0].rearrange("p i g -> p (i g)").unsqueeze(2).broadcast_to(s3), ALU.mult))
                link(V.tensor_tensor(m_q, m_q, gmask[:, 1].rearrange("p i g -> p (i g)").unsqueeze(2).broadcast_to(s3), ALU.add))
                one = largest(sel, TOPK, E)
                link(V.tensor_reduce(sel, one.rearrange("p i k e -> p i e k"), AX.X, ALU.add))
                if b == 1:
                    await_computed(dve, ("ranks", 0))
                V.tensor_copy(sel_bf, sel).then_inc(sel_ready, 1)
                s4 = [P, TB, TOPK, E]
                link(V.tensor_tensor(weighed, one, over(score, s4, 2), ALU.mult))
                link(V.tensor_reduce(recs[:, b * TB:(b + 1) * TB, :, 2], weighed, AX.X, ALU.add))

            def place(b):
                key = ("ranks", b)
                ps = await_result(dve, key)
                for i in range(TB):
                    link(V.tensor_tensor(rank[:, i, :], ps[:, i * E:(i + 1) * E], used[:, :], ALU.add))
                    ins = V.tensor_tensor(used[:, :], ps[:, (TB + i) * E:(TB + i + 1) * E], used[:, :], ALU.add)
                    if i < TB - 1:
                        link(ins)
                    else:
                        link_free(ins, key)
                link(V.tensor_copy(rank_i[:, 0], rank))
                link(V.tensor_scalar(rank_i[:, 1], rank_i[:, 0], 7, None, ALU.arith_shift_right))
                link(V.tensor_scalar(rank_i[:, 0], rank_i[:, 0], P - 1, None, ALU.bitwise_and))
                link(V.tensor_scalar(rank, rank_i[:, 0], float(NCOL), None, ALU.mult))
                link(V.tensor_tensor(rank, rank, rank_i[:, 1], ALU.add))
                link(V.scalar_tensor_tensor(out=rank, in0=over(iota_e[:, :], [P, TB, E], 1), scalar=float(NT), in1=rank,
                                            op0=ALU.mult, op1=ALU.add))
                s4 = [P, TB, TOPK, E]
                link(V.tensor_tensor(weighed, chosen, over(rank, s4, 2), ALU.mult))
                link(V.tensor_reduce(top_f[:, :, 0:TOPK], weighed, AX.X, ALU.add))
                V.tensor_copy(rows_i[:, b * TB:(b + 1) * TB, :], top_f[:, :, 0:TOPK]).then_inc(recs_ready, 1)

            def shared(b):
                for g in range(NG):
                    for m, (a, n) in enumerate(SC):
                        key = ("su", b, g, m)
                        ps = await_result(dve, key)
                        await_read(dve, ("sg", b, g, m))
                        V.tensor_tensor(sT[0:n, m, :], sT[0:n, m, :], ps[0:n, :], ALU.mult).then_inc(free(key), 1)
                    for i in range(g * GT, (g + 1) * GT):
                        t = b * TB + i
                        key = ("sd", b, i)
                        ps = await_result(dve, key)
                        link_free(V.tensor_tensor(sh_tmp, ps[:, 0:C], gb[:, b, :], ALU.mult), key)
                        link(V.tensor_tensor(X[:, t, :], X[:, t, :], sh_tmp, ALU.add))

            attend(0)
            choose(0)
            place(0)
            attend(1)
            choose(1)
            shared(0)
            place(1)
            shared(1)

            shape = [P, E, NT]
            link(V.tensor_tensor(more, used[:, :].unsqueeze(2).broadcast_to(shape),
                                 iota_n[:, :].unsqueeze(1).broadcast_to(shape), ALU.is_gt))
            link(V.tensor_reduce(seg[:, 0, :], more, AX.X, ALU.add))
            link(V.memset(seg[:, 2, :], 1.0))
            link(V.tensor_tensor_scan(seg[:, 1, :], seg[:, 2, :], seg[:, 0, :], 0.0, ALU.mult, ALU.add))
            link(V.tensor_tensor(seg[:, 0, :], seg[:, 1, :], seg[:, 0, :], ALU.subtract))
            link(V.tensor_scalar(seg[:, 2, :], seg[:, 1, :], iota_p[:, 0:1], None, ALU.is_le))
            link(V.tensor_reduce(mapf[:, 0:1], seg[:, 2, :], AX.X, ALU.add))
            link(V.tensor_scalar(mapf[:, 0:1], mapf[:, 0:1], float(E - 1), None, ALU.min))
            link(V.tensor_scalar(seg[:, 3, :], iota_e[:, :], mapf[:, 0:1], None, ALU.is_equal))
            link(V.scalar_tensor_tensor(out=seg[:, 0, :], in0=iota_e[:, :], scalar=float(NT), in1=seg[:, 0, :],
                                        op0=ALU.mult, op1=ALU.subtract))
            link(V.tensor_tensor(seg[:, 3, :], seg[:, 3, :], seg[:, 0, :], ALU.mult))
            link(V.tensor_reduce(mapf[:, 1:2], seg[:, 3, :], AX.X, ALU.add))
            link(V.tensor_tensor(mapf[:, 1:2], mapf[:, 1:2], iota_p[:, 0:1], ALU.add))
            link(V.tensor_tensor(mapf[:, 2:3], iota_p[:, 0:1], seg[:, 1, E - 1:E], ALU.is_ge))
            link(V.scalar_tensor_tensor(out=mapf[:, 1:2], in0=mapf[:, 2:3], scalar=2.0 * P * NT, in1=mapf[:, 1:2],
                                        op0=ALU.mult, op1=ALU.add))
            link(V.tensor_scalar(mapf[:, 1:2], mapf[:, 1:2], float(EMPTY), None, ALU.min))
            link(V.tensor_scalar(seg[:, 3, 0:TURNS], iota_e[:, 0:TURNS], float(R), None, ALU.mult))
            link(V.tensor_scalar(seg[:, 3, 0:TURNS], seg[:, 3, 0:TURNS], seg[:, 1, E - 1:E], None, ALU.is_lt))
            link(V.tensor_reduce(mapf[:, 2:3], seg[:, 3, 0:TURNS], AX.X, ALU.add))
            link(V.memset(map_i, 0))
            V.tensor_scalar(mapf[:, 2:3], mapf[:, 2:3], -2.0, None, ALU.add).then_inc(mapf_ready, 1)
            dve.wait_ge(mapf_ready, 1)
            link(V.tensor_copy(map_i[0:1, 2 * MAP_W:2 * MAP_W + 1], mapf[0:1, 2:3]))
            ps = await_result(dve, ("map",))
            V.tensor_copy(map_i[0:1, 0:2 * MAP_W].rearrange("p (a n) -> p a n", a=2)[:, :, 0:P],
                          ps[0:1, 0:2 * P].rearrange("p (a n) -> p a n", a=2)).then_inc(free(("map",)), 1)
            await_read(dve, ("map",))
            dve.wait_ge(ld_lists, 16)

            def tokens(c, col, turn):
                if not isinstance(turn, int) or turn > 0:
                    dve.wait_ge(gathered[c], 16 * turn)
                V.tensor_copy(tok_i[:, c:c + 1], lists_sb[:, bass.ds(col * 4, 1)]).then_inc(tok_listed, 1)

            def dests(c, col, turn):
                if not isinstance(turn, int) or turn > 0:
                    dve.wait_ge(scattered[c], 16 * turn)
                V.tensor_copy(dest_i[:, c:c + 1], lists_sb[:, bass.ds(col * 4 + 1, 1)])
                V.tensor_copy(pair_w[:, c:c + 1], lists_sb[:, bass.ds(col * 4 + 2, 1)]).then_inc(dest_listed, 1)

            def copy_x(c, n):
                dve.wait_ge(x_turned, n + 1)
                if not isinstance(n, int) or n >= 2:
                    dve.wait_ge(gu_done, n - 1)
                V.tensor_copy(xT[:, c % 2], banks[0][:, 0:C].rearrange("p (k n) -> p k n", k=KC)).then_inc(xT_copied, 1)

            def multiply(c, n):
                dve.wait_ge(silu_done, n + 1)
                if not isinstance(n, int) or n >= 2:
                    dve.wait_ge(act_turned, n - 1)
                V.tensor_tensor(act[:, c % 2, :], act_g[:, c % 2, :], banks[1 + c % 2][:, M:M2], ALU.mult).then_inc(act_done, 1)

            DVE = mybir.EngineType.DVE
            cols = load_values(dve, DVE, 1, 0)
            for c in range(R):
                tokens(c, cols[c], 0)
            dests(0, cols[0], 0)
            copy_x(0, 0)
            copy_x(1, 1)
            multiply(0, 0)

            def step(turn, last):
                cols = load_values(dve, DVE, 1, turn)
                for c in range(R):
                    n = R * turn + c
                    if not last:
                        tokens(c, cols[c + R], turn + 1)
                    if not last or c + 1 < R:
                        dests((c + 1) % R, cols[c + 1], turn + (c + 1) // R)
                    if not last or c + 2 < R:
                        copy_x(c, n + 2)
                    if not last or c + 1 < R:
                        multiply(c + 1, n + 1)

            blocks(dve, step)

            for t in range(NT):
                dve.wait_ge(fetched[t % 4], 16 * (t // 4 + 1))
                if t >= 2:
                    dve.wait_ge(out_ready, t - 1)
                r, s = ring[t % 4], sums[t % 2]
                link(V.tensor_tensor(s, r[:, 0:3, :], r[:, 3:6, :], ALU.add))
                link(V.tensor_tensor(s[:, 0, :], s[:, 0, :], s[:, 1, :], ALU.add))
                V.tensor_tensor(s[:, 0, :], s[:, 0, :], s[:, 2, :], ALU.add).then_inc(summed, 1)

        @block.tensor
        def _(pe):
            mm = nc.tensor.matmul

            def turn(out_ap, in_ap):
                return nc.tensor.transpose(out_ap, in_ap, ident[:, :])

            pe.wait_ge(consts, 10)
            pe.wait_ge(ld_c, 16)
            ps = fill(pe, ("c",))
            for k in range(KC):
                last = nc.tensor.transpose(ps[:, k * B:(k + 1) * B], c_row[:, k * P:(k + 1) * P], ident[0:B, 0:B])
            last.then_inc(full(("c",)), 1)
            pe.wait_ge(ld_mod, 16)
            pe.wait_ge(cs_ready, 1)
            for b in range(B):
                for s in range(2):
                    ps = fill(pe, ("mod", b, s))
                    for k in range(KC):
                        a = 2 * C + s * 2 * C
                        last = mm(ps[:, :], csB[:, k, b, :], wmod_sb[:, k, a:a + 2 * C], start=k == 0, stop=k == KC - 1)
                    last.then_inc(full(("mod", b, s)), 1)
            ps = fill(pe, ("modT",))
            for o in range(2 * KC):
                for k in range(KC):
                    last = mm(ps[:, o * B:(o + 1) * B], wmod_sb[:, k, o * P:(o + 1) * P], csT[:, k, :],
                              start=k == 0, stop=k == KC - 1)
            last.then_inc(full(("modT",)), 1)
            pe.wait_ge(ld_qkv, 16)
            for g in range(2 * KC):
                ps = fill(pe, ("wT", g))
                for o in range(3):
                    last = turn(ps[:, o * P:(o + 1) * P], wqkv_raw[:, (g % 2) * 3 + o, (g // 2) * P:(g // 2 + 1) * P])
                last.then_inc(full(("wT", g)), 1)
            pe.wait_ge(ld_proj, 32)
            for k in range(KC):
                ps = fill(pe, ("wpT", k))
                for o in range(KC):
                    last = turn(ps[:, o * P:(o + 1) * P], wproj_raw[:, o, k * P:(k + 1) * P])
                last.then_inc(full(("wpT", k)), 1)

            def drained_by(key):
                await_read(pe, key)

            def keys_values(b):
                pend = []

                def outer():
                    i = pend.pop(0)
                    t = b * TB + i
                    drained_by(("kv", b, i))
                    for k in range(KC):
                        if i == 0:
                            fill(pe, ("vk", b, k))
                        last = mm(of(("vk", b, k))[:, 0:HH * VE], kk[:, t % 2, k * P:(k + 1) * P],
                                  vv[:, t % 2, k * HH:(k + 1) * HH, :], start=i == 0, stop=i == TB - 1)
                        if i == TB - 1:
                            last.then_inc(full(("vk", b, k)), 1)
                    if i < TB - 1:
                        last.then_inc(kv_used, 1)

                for g in range(NG):
                    keys = [("hT", b, g, k) for k in range(KC)]
                    for k in range(KC):
                        fill(pe, keys[k])
                    for i in range(GT):
                        t = b * TB + g * GT + i
                        pe.wait_ge(xn_ready, t + 1)
                        for k in range(KC):
                            last = turn(of(keys[k])[:, i * P:(i + 1) * P], xn[:, t, k * P:(k + 1) * P])
                            if i == GT - 1:
                                last.then_inc(full(keys[k]), 1)
                    for k in range(KC):
                        drained_by(keys[k])
                    for m in range(KC):
                        key = ("q", b, g, m)
                        ps = fill(pe, key)
                        if b == 0 and g == 0 and m == 0:
                            drained_by(("wT", 2 * KC - 1))
                            drained_by(("wT", 2 * KC - 2))
                        for k in range(KC):
                            last = mm(ps[:, :], wT[:, k, m * P:(m + 1) * P], hT[:, k, :], start=k == 0, stop=k == KC - 1)
                        last.then_inc(full(key), 1)
                    for i in range(GT):
                        key = ("kv", b, g * GT + i)
                        ps = fill(pe, key)
                        for k in range(KC):
                            last = mm(ps[:, :], hT[:, k, i * P:(i + 1) * P], wT[:, k, C:3 * C], start=k == 0, stop=k == KC - 1)
                        last.then_inc(full(key), 1)
                        if pend:
                            outer()
                        pend.append(g * GT + i)
                    outer()

            def attend(b):
                for k in range(KC):
                    drained_by(("vk", b, k))
                if b == 0:
                    pe.wait_ge(wpT_ready, 1)
                for g in range(NG):
                    for k in range(KC):
                        for a, name in enumerate(("num", "den")):
                            key = (name, b, g, k)
                            ps = fill(pe, key)
                            last = mm(ps[:, :], nd[:, k, a, :], qT[:, k, g * W:(g + 1) * W], start=True, stop=True)
                            last.then_inc(full(key), 1)
                    for k in range(KC):
                        drained_by(("num", b, g, k))
                    for i in range(GT):
                        key = ("proj", b, g * GT + i)
                        ps = fill(pe, key)
                        for k in range(KC):
                            last = mm(ps[:, 0:C], oT[:, k, i * P:(i + 1) * P], wpT[:, b, k, :], start=k == 0, stop=k == KC - 1)
                        last.then_inc(full(key), 1)

            def turn_h2(b):
                for g in range(NG):
                    keys = [("h2T", b, g, k) for k in range(KC)]
                    for k in range(KC):
                        fill(pe, keys[k])
                    for i in range(GT):
                        pe.wait_ge(h2_ready, b * TB + g * GT + i + 1)
                        for k in range(KC):
                            last = turn(of(keys[k])[:, i * P:(i + 1) * P], h2[:, g * GT + i, k * P:(k + 1) * P])
                            if i == GT - 1:
                                last.then_inc(full(keys[k]), 1)
                if b == 0:
                    pe.wait_ge(ld_route, 32)
                key = ("router", b)
                ps = fill(pe, key)
                for g in range(NG):
                    for k in range(KC):
                        drained_by(("h2T", b, g, k))
                    for i in range(g * GT, (g + 1) * GT):
                        for k in range(KC):
                            last = mm(ps[:, i * E:(i + 1) * E], h2T[:, b, k, i * P:(i + 1) * P], router[:, k, :],
                                      start=k == 0, stop=k == KC - 1)
                last.then_inc(full(key), 1)

            def ranks(b):
                pe.wait_ge(sel_ready, b + 1)
                ps = fill(pe, ("ranks", b))
                w = TB * E
                moving = sel_bf.rearrange("p i e -> p (i e)")
                mm(ps[:, 0:w], tri[:, :], moving, start=True, stop=True)
                mm(ps[:, w:2 * w], ones_bf[:, :], moving, start=True, stop=True).then_inc(full(("ranks", b)), 1)

            def shared(b):
                if b == 0:
                    pe.wait_ge(ld_sh, 16 * (2 + len(SC)))
                for g in range(NG):
                    for m, (a, n) in enumerate(SC):
                        for s, name in enumerate(("sg", "su")):
                            key = (name, b, g, m)
                            ps = fill(pe, key)
                            for k in range(KC):
                                last = mm(ps[0:n, :], sh_gu[:, s, k, a:a + n], h2T[:, b, k, g * W:(g + 1) * W],
                                          start=k == 0, stop=k == KC - 1)
                            last.then_inc(full(key), 1)
                    for m in range(len(SC)):
                        drained_by(("su", b, g, m))
                    for i in range(GT):
                        key = ("sd", b, g * GT + i)
                        ps = fill(pe, key)
                        for m, (a, n) in enumerate(SC):
                            last = mm(ps[:, 0:C], sT[0:n, m, i * P:(i + 1) * P], sh_dn[0:n, m, :],
                                      start=m == 0, stop=m == len(SC) - 1)
                        last.then_inc(full(key), 1)

            keys_values(0)
            attend(0)
            turn_h2(0)
            keys_values(1)
            ranks(0)
            attend(1)
            turn_h2(1)
            shared(0)
            ranks(1)
            shared(1)
            pe.wait_ge(mapf_ready, 1)
            ps = fill(pe, ("map",))
            for a in range(2):
                last = mm(ps[0:1, a * P:(a + 1) * P], mapf[:, a:a + 1], ident[:, :], start=True, stop=True)
            last.then_inc(full(("map",)), 1)

            for bank in range(8):
                pe.wait_ge(drained[bank], uses[bank])
            pe.wait_ge(ld_early, 16 * EARLY // 8 * 2 * KC)
            pe.wait_ge(ld_late, 16 * (2 + 2 * KC))

            def turn_x(s, n, turn):
                pe.wait_ge(gathered[s], 16 * (turn + 1))
                if not isinstance(n, int) or n >= 1:
                    pe.wait_ge(xT_copied, n)
                for k in range(KC):
                    last = nc.tensor.transpose(banks[0][:, k * P:(k + 1) * P], xg[:, s, k * P:(k + 1) * P], ident[:, :])
                last.then_inc(x_turned, 1)

            def gate_and_up(c, n, e):
                pe.wait_ge(xT_copied, n + 1)
                if not isinstance(n, int) or n >= 2:
                    pe.wait_ge(act_done, n - 1)
                for k in range(KC):
                    last = mm(banks[1 + c % 2][:, 0:M2], xT[:, c % 2, k, :],
                              gate_up[:, bass.ds(e * (KC * M2) + k * M2, M2)], start=k == 0, stop=k == KC - 1)
                last.then_inc(gu_done, 1)

            def turn_act(c, n):
                pe.wait_ge(act_done, n + 1)
                if not isinstance(n, int) or n >= 1:
                    pe.wait_ge(aT_copied, n)
                for m in range(2):
                    last = nc.tensor.transpose(banks[3][0:KD, m * P:(m + 1) * P], act[:, c % 2, m * KD:(m + 1) * KD], ident[:, :])
                last.then_inc(act_turned, 1)

            def down_rows(c, n, e):
                pe.wait_ge(aT_copied, n + 1)
                if not isinstance(n, int) or n >= 2:
                    pe.wait_ge(y_scaled, n - 1)
                for m in range(2):
                    last = mm(banks[4 + c % 2][:, 0:C], aT[0:KD, c % 2, m, :],
                              down[0:KD, bass.ds(e * C + m * E * C, C)], start=m == 0, stop=m == 1)
                last.then_inc(y_done, 1)

            turn_x(0, 0, 0)
            turn_x(1, 1, 0)
            PE = mybir.EngineType.PE
            gate_and_up(0, 0, load_values(pe, PE, 0, 0)[0])

            def step(turn, last):
                experts = load_values(pe, PE, 0, turn)
                for c in range(R):
                    n = R * turn + c
                    turn_act(c, n)
                    if not last or c + 2 < R:
                        turn_x((c + 2) % R, n + 2, turn + (c + 2) // R)
                    if not last or c + 1 < R:
                        gate_and_up(c + 1, n + 1, experts[c + 1])
                    down_rows(c, n, experts[c])

            blocks(pe, step)


_INS = ['L0_attn_x', 'L0_attn_w_qkv', 'L0_attn_w_proj', 'L0_attn_b_proj', 'L0_ffn_w_router', 'L0_ffn_corr_bias',
        'L0_ffn_gate_w', 'L0_ffn_up_w', 'L0_ffn_down_w', 'L0_ffn_sh_gate_w', 'L0_ffn_sh_up_w', 'L0_ffn_sh_down_w',
        'L0_c', 'L0_wmod']


def kernel(**inputs):
    import numpy as _np
    import concourse.bacc as _bacc
    from concourse import mybir as _mybir
    from concourse.bass_utils import run_bass_kernel_spmd as _run

    nc = _bacc.Bacc("TRN2", target_bir_lowering=False, num_devices=1)
    arrays, args = {}, []
    for name in _INS:
        a = _np.ascontiguousarray(inputs[name])
        arrays[f"in_{name}"] = a
        args.append(nc.dram_tensor(f"in_{name}", a.shape, _mybir.dt.from_np(a.dtype), kind="ExternalInput").ap())
    shape = inputs["L0_attn_x"].shape
    args.append(nc.dram_tensor("out_0", shape, _mybir.dt.float32, kind="ExternalOutput").ap())
    build_block(nc, *args)
    r = _run(nc, [arrays], core_ids=[0])
    return r.results[0]["out_0"]
```

```python
def build_block(nc, x_in, w_qkv, w_proj, b_proj, w_router, corr_bias, gate_w, up_w, down_w,
                sh_gate_w, sh_up_w, sh_down_w, cond, w_mod, out):
    import concourse.bass as bass
    from concourse import mybir
    from contextlib import ExitStack

    f32, i32, u32, bf16 = mybir.dt.float32, mybir.dt.int32, mybir.dt.uint32, mybir.dt.bfloat16
    ALU, ACT, AX = mybir.AluOpType, mybir.ActivationFunctionType, mybir.AxisListType

    P = 128
    B, N, C = x_in.shape
    T = B * N
    NT = T // P
    TB = NT // B
    GT = 4
    NG = TB // GT
    W = GT * P
    KC = C // P
    HD = 32
    NH = C // HD
    HH = NH // KC
    VE = HD + 1
    E, _, M = gate_w.shape
    M2 = 2 * M
    KD = M // 2
    SM = sh_gate_w.shape[1]
    SC = [(a, min(P, SM - a)) for a in range(0, SM, P)]
    TOPK, G, TOPG = 6, 8, 4
    EG = E // G
    NBLK = (T * TOPK - E) // P + E + 1
    TURNS = -(-NBLK // 4)
    FEWEST = T * TOPK // P // 4 - 1
    MAP_W = P + 8
    NCOL = E * NT + 1
    EMPTY = NCOL - 1
    LN_EPS, DIV_EPS, GUARD = 1e-5, 1e-15, 0.25
    LOW = -3.0e38

    x_v = x_in.rearrange("b (i p) c -> p (b i) c", p=P)
    out_v = out.rearrange("b (i p) c -> p (b i) c", p=P)

    ctx = ExitStack()
    with ctx:
        def sb(name, shape, dt=f32):
            return ctx.enter_context(nc.sbuf_tensor(name, shape, dt))

        def sem(name):
            return ctx.enter_context(nc.semaphore(name))

        def shared_part(region, width):
            at = [0]

            def take(n):
                a = at[0]
                at[0] += n
                assert at[0] <= width, (at[0], width)
                return region[:, a:a + n]
            return take

        h2_dram = nc.dram_tensor("h2_rows", (T, C), f32).ap()
        lists = nc.dram_tensor("pair_lists", (P * NCOL, 4), f32).ap()
        token_sums = [nc.dram_tensor(f"token_sums{a}", (T, C), f32).ap() for a in range(2)]
        h2_tiles = h2_dram.rearrange("(i p) c -> p i c", p=P)
        lists_v = lists.rearrange("(p n) w -> p (n w)", p=P)
        sums_v = [a.rearrange("(i p) c -> p i c", p=P) for a in token_sums]

        EARLY = 24
        gate_up = sb("gate_up", [P, E * KC * M2])
        gu_v = gate_up[:, :].rearrange("p (e k m) -> p e k m", e=E, k=KC)
        down = sb("down", [P, 2 * E * C])
        dn_v = down[:, :].rearrange("p (m f) -> p m f", m=2)
        X = sb("X", [P, NT, C])
        tok_buf = sb("tok_buf", [P, NT * C])
        xn = tok_buf[:, :].rearrange("p (i c) -> p i c", i=NT)
        h2T = tok_buf[:, :].rearrange("p (b k n) -> p b k n", b=B, k=KC)
        sh_gu = sb("sh_gu", [P, 2, KC, SM])
        sh_dn = sb("sh_dn", [P, len(SC), C])
        router = sb("router", [P, KC, E])
        bias_bc = sb("bias_bc", [P, E])
        gb = sb("gb", [P, B, C])
        lists_sb = sb("lists_sb", [P, NCOL * 4])
        sT = lists_sb[:, 0:len(SC) * W].rearrange("p (m n) -> p m n", m=len(SC))
        sh_tmp = lists_sb[:, len(SC) * W:len(SC) * W + C]
        recs = sb("recs", [P, NT, TOPK, 4])
        rows_i = sb("rows_i", [P, NT, TOPK], i32)
        ident = sb("ident", [P, P])
        tri = sb("tri", [P, P], bf16)
        ones_bf = sb("ones_bf", [P, P], bf16)
        iota_e = sb("iota_e", [P, E])
        iota_p = sb("iota_p", [P, 1])
        used = sb("used", [P, E])
        stats = sb("stats", [P, NT, 6])
        mv = sb("mv", [P, NT, 2])
        mv2 = sb("mv2", [P, NT, 2])
        rstd = sb("rstd", [P, NT])
        rstd2 = sb("rstd2", [P, NT])
        half = sb("half", [P, TB])
        modT = sb("modT", [P, 4, B])
        mapf = sb("mapf", [P, 4])
        iota_n = sb("iota_n", [P, NT])

        part = shared_part(down, 2 * E * C)
        wmod_sb = part(KC * 6 * C).rearrange("p (k n) -> p k n", k=KC)
        route_tmp = wmod_sb
        c_row = part(C)[0:B, :]
        csT = part(KC * B).rearrange("p (k b) -> p k b", k=KC)
        csB = part(KC * B * P).rearrange("p (k b n) -> p k b n", k=KC, b=B)
        wqkv_raw = part(3 * KC * C).rearrange("p (o c) -> p o c", o=3 * KC)
        wproj_raw = part(KC * C).rearrange("p (o c) -> p o c", o=KC)
        wT = part(KC * 3 * C).rearrange("p (k o) -> p k o", k=KC)
        wpT = part(B * KC * C).rearrange("p (b k o) -> p b k o", b=B, k=KC)
        rows = part(B * 4 * C).rearrange("p (b r c) -> p b r c", b=B, r=4)
        bga = part(B * C).rearrange("p (b c) -> p b c", b=B)
        hT = part(KC * N // 2).rearrange("p (k n) -> p k n", k=KC)
        qT = part(KC * N).rearrange("p (k n) -> p k n", k=KC)
        kk = part(2 * C).rearrange("p (s c) -> p s c", s=2)
        vv = part(2 * NH * VE).rearrange("p (s h e) -> p s h e", s=2, h=NH)
        nd = part(KC * HH * VE).rearrange("p (k n) -> p k n", k=KC)
        rden = part(2 * NH).rearrange("p (s h) -> p s h", s=2)
        o = wqkv_raw[:, 0:2, :]
        oT = part(2 * KC * P).rearrange("p (s k n) -> p s k n", s=2, k=KC)

        part = shared_part(gate_up[:, EARLY * KC * M2:], (E - EARLY) * KC * M2)
        h2 = part(TB * C).rearrange("p (i c) -> p i c", i=TB)
        chosen = part(TB * TOPK * E).rearrange("p (i k e) -> p i k e", i=TB, k=TOPK)
        score = part(TB * E).rearrange("p (i e) -> p i e", i=TB)
        sfc = part(TB * E).rearrange("p (i e) -> p i e", i=TB)
        sel = part(TB * E).rearrange("p (i e) -> p i e", i=TB)
        sel_bf = part(TB * E // 2).bitcast(bf16).rearrange("p (i e) -> p i e", i=TB)
        rank = part(TB * E).rearrange("p (i e) -> p i e", i=TB)
        tmp = wmod_sb[:, :, :].rearrange("p k n -> p (k n)")
        weighed = tmp[:, 0:TB * TOPK * E].rearrange("p (i k e) -> p i k e", i=TB, k=TOPK)
        at = TB * TOPK * E
        rank_i = tmp[:, at:at + 2 * TB * E].bitcast(i32).rearrange("p (a i e) -> p a i e", a=2, i=TB)
        at += 2 * TB * E
        pair = tmp[:, at:at + 4 * TB * G].rearrange("p (a i g) -> p a i g", a=4, i=TB)
        at += 4 * TB * G
        gs = tmp[:, at:at + TB * G].rearrange("p (i g) -> p i g", i=TB)
        at += TB * G
        gmask = tmp[:, at:at + 2 * TB * G].rearrange("p (a i g) -> p a i g", a=2, i=TB)
        at += 2 * TB * G
        top = tmp[:, at:at + TB * 8].rearrange("p (i k) -> p i k", i=TB)
        at += TB * 8
        top_f = tmp[:, at:at + TB * 8].rearrange("p (i k) -> p i k", i=TB)
        at += TB * 8
        top_i = tmp[:, at:at + TB * 8].bitcast(u32).rearrange("p (i k) -> p i k", i=TB)
        at += TB * 8
        assert at <= KC * 6 * C

        part = shared_part(tok_buf, NT * C // 2)
        R = 4
        xg = part(R * C).rearrange("p (s c) -> p s c", s=R)
        xT = part(2 * C).rearrange("p (s k n) -> p s k n", s=2, k=KC)
        aT = part(2 * 2 * P).rearrange("p (s m n) -> p s m n", s=2, m=2)
        part = shared_part(tok_buf[:, NT * C // 2:], NT * C // 2)
        yw = part(R * C).rearrange("p (s c) -> p s c", s=R)
        act_g = part(2 * M).rearrange("p (s m) -> p s m", s=2)
        act = part(2 * M).rearrange("p (s m) -> p s m", s=2)
        map_i = part(2 * MAP_W + 1)[0:1, :].bitcast(i32)
        more = tmp[:, 0:E * NT].rearrange("p (e n) -> p e n", e=E)
        seg = tmp[:, E * NT:(NT + 4) * E].rearrange("p (a e) -> p a e", a=4)
        tok_i = sb("tok_i", [P, R], i32)
        dest_i = sb("dest_i", [P, R], i32)
        pair_w = sb("pair_w", [P, R])
        sums = gate_up[:, 0:2 * NT * C].rearrange("p (a i c) -> p a i c", a=2, i=NT)

        banks = [ctx.enter_context(nc.psum_tensor(f"bank{i}", [P, 512], f32)) for i in range(8)]

        filled = [sem(f"bank{i}_filled") for i in range(8)]
        drained = [sem(f"bank{i}_drained") for i in range(8)]
        ld_c, ld_mod, ld_qkv, ld_proj, ld_route, ld_sh = (sem("ld_" + n) for n in ("c", "mod", "qkv", "proj", "route", "shared"))
        ld_x = [sem(f"ld_x{i}") for i in range(NT // GT)]
        ld_early, ld_late, ld_lists = sem("ld_early_weights"), sem("ld_late_weights"), sem("ld_lists")
        consts = sem("constants_ready")
        pool_passed = sem("pool_passed_waits")
        dve_own, pool_own = sem("dve_own_steps"), sem("pool_own_steps")
        var_ready, rstd_ready, xn_ready, xb_ready = (sem(n) for n in ("var_ready", "rstd_ready", "xn_ready", "xb_ready"))
        cs_ready, wpT_ready, kv_used = (
            sem(n) for n in ("csB_ready", "gated_projection_ready", "keys_values_used"))
        var2_ready, rstd2_ready, xn2_ready, h2_ready, h2_stored = (
            sem(n) for n in ("var2_ready", "rstd2_ready", "xn2_ready", "h2_ready", "h2_stored"))
        sel_ready, recs_ready, lists_clear, listed = (
            sem(n) for n in ("chosen_ready", "records_ready", "lists_clear", "listed"))
        base_ready, zero_ready, sums_clear = sem("base_ready"), sem("zeros_ready"), sem("token_sums_clear")
        mapf_ready = sem("map_columns_ready")
        tok_listed, dest_listed = sem("block_tokens_ready"), sem("block_dests_ready")
        gathered = [sem(f"gathered{s}") for s in range(R)]
        scattered = [sem(f"scattered{s}") for s in range(R)]
        x_turned, xT_copied, gu_done, silu_done, act_done, act_turned, aT_copied, y_done, y_scaled = (
            sem(n) for n in ("x_turned", "xT_copied", "gate_up_done", "silu_done", "act_done", "act_turned", "aT_copied", "y_done", "y_scaled"))
        fetched = [sem(f"sums_fetched{g}") for g in range(NT // GT)]
        out_ready, stored = sem("out_ready"), sem("out_stored")

        use = {}
        uses = [0] * 8

        def plan(key, bank):
            uses[bank] += 1
            use[key] = bank, uses[bank]

        def plan_modulation():
            for b in range(B):
                for s in range(2):
                    plan(("mod", b, s), (2 * b + s) % 2)
            for k in range(KC):
                plan(("wpT", k), 2 + k)

        def plan_head(b, g):
            for k in range(KC):
                plan(("hT", b, g, k), k)
            for k in range(KC):
                plan(("q", b, g, k), 2 + k)

        def plan_tiles(b, g):
            for i in range(GT):
                plan(("kv", b, g * GT + i), 4 + i % 2)
            if g == NG - 1:
                for k in range(KC):
                    plan(("vk", b, k), 6 + k)

        def plan_attend(b):
            for i in range(TB):
                plan(("o", b, i), 2 + i % 2)
                plan(("oT", b, i), i % 2)
                plan(("proj", b, i), 4 + i % 2)

        def plan_turn(b):
            for g in range(NG):
                for k in range(KC):
                    plan(("h2T", b, g, k), k)
            plan(("router", b), 2)

        def plan_ranks(b):
            plan(("ranks", b), 3)

        def plan_shared(b):
            for g in range(NG):
                for m in range(len(SC)):
                    plan(("sg", b, g, m), 2 * (m % 2))
                    plan(("su", b, g, m), 2 * (m % 2) + 1)
                for i in range(GT):
                    plan(("sd", b, g * GT + i), 4 + i % 2)

        plan(("c",), 7)
        for g in range(2 * KC):
            plan(("wT", g), 3 + g % 2)
        plan(("modT",), 2)
        plan_head(0, 0)
        plan_tiles(0, 0)
        plan_modulation()
        plan_head(0, 1)
        plan_tiles(0, 1)
        plan_attend(0)
        plan_head(1, 0)
        plan_turn(0)
        plan_tiles(1, 0)
        plan_head(1, 1)
        plan_ranks(0)
        plan_tiles(1, 1)
        plan_attend(1)
        plan_turn(1)
        plan_ranks(1)
        plan_shared(0)
        plan_shared(1)
        plan(("map",), 6)

        def of(key):
            return banks[use[key][0]]

        def fill(pe, key):
            bank, n = use[key]
            if n > 1:
                pe.wait_ge(drained[bank], n - 1)
            return banks[bank]

        def await_result(eng, key):
            bank, n = use[key]
            eng.wait_ge(filled[bank], n)
            return banks[bank]

        def full(key):
            return filled[use[key][0]]

        def free(key):
            return drained[use[key][0]]

        def await_computed(eng, key):
            eng.wait_ge(full(key), use[key][1])

        def await_read(eng, key):
            eng.wait_ge(free(key), use[key][1])

        def wait(eng, s, value):
            if not isinstance(value, int) or value > 0:
                eng.wait_ge(s, value)

        def first(n):
            return isinstance(n, int) and n == 0

        def load_last_turn(eng):
            return 1 + eng.value_load(map_i[0:1, 2 * MAP_W:2 * MAP_W + 1], min_val=FEWEST - 1, max_val=TURNS - 2)

        def load_values(eng, which, section, turn, first):
            _, values = nc.values_load_multi_w_load_instructions(
                map_i[0:1, bass.ds(section * MAP_W + 1 + first + R * turn, 2 * R)], engines=(which,),
                min_val=0, max_val=(E - 1, EMPTY)[section],
                skip_runtime_bounds_check_because="the map's entries are clamped where they are made")
            return values

        def blocks(eng, step):
            last_turn = load_last_turn(eng)
            step(0, False)
            with eng.Fori(1, TURNS - 1) as turn:
                with eng.If(turn < last_turn):
                    step(turn, False)
            step(last_turn, True)

        block = ctx.enter_context(nc.Block())

        @block.sync
        def _(sp):
            sp.dma_start(c_row, cond).then_inc(ld_c, 16)
            sp.dma_start(wmod_sb, w_mod.rearrange("(k p) n -> p k n", p=P)).then_inc(ld_mod, 16)
            sp.dma_start(X[:, 0:GT, :], x_v[:, 0:GT, :]).then_inc(ld_x[0], 16)
            sp.dma_start(wqkv_raw, w_qkv.rearrange("(o p) c -> p o c", p=P)).then_inc(ld_qkv, 16)
            sp.dma_start(wproj_raw, w_proj.rearrange("(o p) c -> p o c", p=P)).then_inc(ld_proj, 16)
            sp.dma_start(bga[:, 0, :], b_proj.partition_broadcast(P)).then_inc(ld_proj, 16)
            for g in range(1, NT // GT):
                sp.dma_start(X[:, g * GT:(g + 1) * GT, :], x_v[:, g * GT:(g + 1) * GT, :]).then_inc(ld_x[g], 16)
            sp.dma_start(router[:, :, :], w_router.rearrange("(k p) e -> p k e", p=P)).then_inc(ld_route, 16)
            sp.dma_start(bias_bc[:, :], corr_bias.partition_broadcast(P)).then_inc(ld_route, 16)
            for a, w in enumerate((sh_gate_w, sh_up_w)):
                sp.dma_start(sh_gu[:, a, :, :], w.rearrange("(k p) m -> p k m", p=P)).then_inc(ld_sh, 16)
            for m, (a, n) in enumerate(SC):
                sp.dma_start(sh_dn[0:n, m, :], sh_down_w[a:a + n, :]).then_inc(ld_sh, 16)
            sp.wait_ge(zero_ready, 1)
            for a in range(2):
                sp.dma_start(sums_v[a], h2[:, 0:1, :].broadcast_to([P, NT, C])).then_inc(sums_clear, 16)
            sp.wait_ge(consts, 7)
            sp.dma_start(lists_v, lists_sb[:, :]).then_inc(lists_clear, 16)

            def load_gate_up(e0, e1, s):
                for a, w in enumerate((gate_w, up_w)):
                    for k in range(KC):
                        sp.dma_start(gu_v[:, e0:e1, k, a * M:(a + 1) * M],
                                     w[e0:e1, k * P:(k + 1) * P, :].rearrange("e p m -> p e m")).then_inc(s, 16)

            for e in range(0, EARLY, 8):
                load_gate_up(e, e + 8, ld_early)
            for b in range(B):
                for g in range(NG):
                    sp.wait_ge(h2_ready, b * TB + (g + 1) * GT)
                    t = b * TB + g * GT
                    sp.dma_start(h2_tiles[:, t:t + GT, :], h2[:, g * GT:(g + 1) * GT, :]).then_inc(h2_stored, 16)
            sp.wait_ge(h2_stored, 16 * B * NG)
            await_computed(sp, ("h2T", B - 1, NG - 1, KC - 1))
            sp.wait_ge(recs_ready, B)
            sp.wait_ge(mapf_ready, 1)
            for m in range(2):
                sp.dma_start(dn_v[0:KD, m, :].rearrange("p (e c) -> p e c", e=E),
                             down_w[:, m * KD:(m + 1) * KD, :].rearrange("e p c -> p e c")).then_inc(ld_late, 16)
            load_gate_up(EARLY, E, ld_late)
            sp.wait_ge(listed, 16 * NT * TOPK)
            sp.wait_ge(base_ready, NT)
            sp.dma_start(lists_sb[:, :], lists_v).then_inc(ld_lists, 16)
            await_read(sp, ("map",))
            last_turn = load_last_turn(sp)
            for s in range(R):
                sp.wait_ge(scattered[s], 16 * last_turn + 16)
            for g in range(NT // GT):
                tiles = slice(g * GT, (g + 1) * GT)
                for a in range(2):
                    sp.dma_start(sums[:, a, tiles, :], sums_v[a][:, tiles, :]).then_inc(fetched[g], 16)
            for g in range(NT // GT):
                tiles = slice(g * GT, (g + 1) * GT)
                sp.wait_ge(out_ready, g + 1)
                sp.dma_start(out_v[:, tiles, :], X[:, tiles, :]).then_inc(stored, 16)
            sp.wait_ge(stored, 16 * NT // GT)

        @block.gpsimd
        def _(pool):
            done = [0]

            def link(ins):
                done[0] += 1
                ins.then_inc(pool_own, 1)
                pool.wait_ge(pool_own, done[0])

            nc.gpsimd.memset(h2[:, 0, :], 0.0).then_inc(zero_ready, 1)
            link(nc.gpsimd.memset(ident[:, :], 0.0))
            nc.gpsimd.affine_select(out=ident[:, :], in_=ident[:, :], compare_op=ALU.not_equal, fill=1.0,
                                    base=0, pattern=[[-1, P]], channel_multiplier=1).then_inc(consts, 1)
            nc.gpsimd.memset(half[:, :], -0.5).then_inc(consts, 1)
            link(nc.gpsimd.memset(ones_bf[:, :], 1.0))
            nc.gpsimd.affine_select(out=tri[:, :], in_=ones_bf[:, :], compare_op=ALU.is_gt, fill=0.0,
                                    base=0, pattern=[[1, P]], channel_multiplier=-1).then_inc(consts, 1)
            nc.gpsimd.iota(iota_e[:, :], [[1, E]], base=0, channel_multiplier=0,
                           allow_small_or_imprecise_dtypes=True).then_inc(consts, 1)
            nc.gpsimd.iota(iota_p[:, :], [[1, 1]], base=0, channel_multiplier=1,
                           allow_small_or_imprecise_dtypes=True).then_inc(consts, 1)
            nc.gpsimd.memset(vv[:, :, :, HD:VE], 1.0).then_inc(consts, 1)
            link(nc.gpsimd.memset(lists_sb[:, :], 0.0))
            nc.gpsimd.iota(lists_sb[:, :].rearrange("p (n w) -> p n w", w=4)[:, :, 1:2], [[0, NCOL]],
                           base=T, channel_multiplier=1,
                           allow_small_or_imprecise_dtypes=True).then_inc(consts, 1)
            link(nc.gpsimd.memset(recs[:, :, :, :], 0.0))
            nc.gpsimd.iota(recs[:, :, :, 0], [[P, NT], [0, TOPK]], base=0, channel_multiplier=1,
                           allow_small_or_imprecise_dtypes=True)
            nc.gpsimd.iota(recs[:, :, :, 1], [[P, NT], [0, TOPK]], base=0, channel_multiplier=1,
                           allow_small_or_imprecise_dtypes=True).then_inc(consts, 1)
            nc.gpsimd.memset(used[:, :], 0.0)
            nc.gpsimd.iota(iota_n[:, :], [[P, NT]], base=0, channel_multiplier=0,
                           allow_small_or_imprecise_dtypes=True).then_inc(consts, 1)
            nc.gpsimd.memset(nd, 0.0).then_inc(consts, 1)

            def power(out_ap, var_ap, n):
                link(nc.gpsimd.tensor_scalar(out_ap, var_ap, LN_EPS, None, ALU.add))
                return nc.gpsimd.tensor_tensor(out_ap, out_ap, half[:, 0:n], ALU.pow)

            pool.wait_ge(consts, 10)
            for g in range(NT // GT):
                a, z = g * GT, (g + 1) * GT
                pool.wait_ge(var_ready, z)
                power(rstd[:, a:z], mv[:, a:z, 1], GT).then_inc(rstd_ready, 1)
            pool.wait_ge(wpT_ready, 1)
            for t in range(NT):
                pool.wait_ge(xn_ready, t + 1)
                nc.gpsimd.tensor_tensor(X[:, t, :], X[:, t, :], bga[:, t // TB, :], ALU.add).then_inc(xb_ready, 1)

            def second_deviation(b, g):
                a = b * TB + g * GT
                pool.wait_ge(var2_ready, a + GT)
                power(rstd2[:, a:a + GT], mv2[:, a:a + GT, 1], GT).then_inc(rstd2_ready, 1)

            def list_pairs(a, z):
                pool.wait_ge(recs_ready, a // TB + 1)
                if a == 0:
                    pool.wait_ge(lists_clear, 16)
                for t in range(a, z):
                    for k in range(TOPK):
                        nc.gpsimd.indirect_dma_start(
                            out=lists, out_offset=bass.IndirectOffsetOnAxis(ap=rows_i[:, t, k:k + 1], axis=0),
                            in_=recs[:, t, k, :], in_offset=None).then_inc(listed, 16)

            second_deviation(0, 0)
            second_deviation(0, 1)
            list_pairs(0, 2)
            second_deviation(1, 0)
            list_pairs(2, 3)
            second_deviation(1, 1)
            list_pairs(3, TB)
            list_pairs(TB, NT)

            pool.wait_ge(h2_stored, 16 * B * NG)
            await_computed(pool, ("sd", 0, TB - 1))

            await_read(pool, ("map",))

            def fetch(s):
                nc.gpsimd.indirect_dma_start(
                    out=xg[:, s, :], out_offset=None, in_=h2_dram,
                    in_offset=bass.IndirectOffsetOnAxis(ap=tok_i[:, s:s + 1], axis=0)).then_inc(gathered[s], 16)

            for s in range(R):
                pool.wait_ge(tok_listed, s + 1)
                fetch(s)

            def gather_next(c, turn):
                pool.wait_ge(tok_listed, R * turn + R + c + 1)
                pool.wait_ge(x_turned, R * turn + c + 1)
                pool.sem_inc(pool_passed, 1)
                fetch(c)

            def scatter(c, n, turns):
                pool.wait_ge(y_scaled, n + 1)
                wait(pool, scattered[(c - 2) % R], 16 * turns)
                pool.sem_inc(pool_passed, 1)
                nc.gpsimd.indirect_dma_start(
                    out=token_sums[c % 2], out_offset=bass.IndirectOffsetOnAxis(ap=dest_i[:, c:c + 1], axis=0),
                    in_=yw[:, c, :], in_offset=None, bounds_check=T - 1, oob_is_err=False,
                    compute_op=ALU.add).then_inc(scattered[c], 16)

            def step(turn, last):
                for c in range(R):
                    n = R * turn + c
                    if not last:
                        gather_next(c, turn)
                    if not first(n):
                        scatter((c - 1) % R, n - 1, turn + (c == R - 1))
                    if last and c == R - 1:
                        scatter(c, n, turn + 1)

            blocks(pool, step)

        @block.scalar
        def _(act_e):
            ps = await_result(act_e, ("c",))
            nc.scalar.activation(csT, ps[:, 0:KC * B].rearrange("p (k b) -> p k b", k=KC),
                                 ACT.Silu).then_inc(free(("c",)), 1)

            for g in range(2 * KC):
                key = ("wT", g)
                ps = await_result(act_e, key)
                n = 3 * C // 2
                nc.scalar.activation(wT[:, g // 2, (g % 2) * n:(g % 2 + 1) * n], ps[:, 0:n], ACT.Copy).then_inc(free(key), 1)

            def head(b, g):
                for k in range(KC):
                    key = ("hT", b, g, k)
                    ps = await_result(act_e, key)
                    if b == 0 and g == 0 and k == 0:
                        await_read(act_e, ("modT",))
                    nc.scalar.activation(hT[:, k, :], ps[:, :], ACT.Identity, bias=modT[:, k, b:b + 1],
                                         scale=modT[:, KC + k, b:b + 1]).then_inc(free(key), 1)
                if b >= 1 and g == 0:
                    await_computed(act_e, ("o", b - 1, TB - 1))
                for k in range(KC):
                    key = ("q", b, g, k)
                    ps = await_result(act_e, key)
                    nc.scalar.activation(qT[:, k, g * W:(g + 1) * W], ps[:, :], ACT.Relu).then_inc(free(key), 1)

            def tiles(b, g):
                for i in range(g * GT, (g + 1) * GT):
                    t = b * TB + i
                    key = ("kv", b, i)
                    ps = await_result(act_e, key)
                    if t >= 2:
                        if (t - 2) % TB == TB - 1:
                            await_computed(act_e, ("vk", (t - 2) // TB, KC - 1))
                        else:
                            act_e.wait_ge(kv_used, t - 1 - (t - 2) // TB)
                    if t == 0:
                        act_e.wait_ge(consts, 10)
                    nc.scalar.activation(kk[:, t % 2, :], ps[:, 0:C], ACT.Relu)
                    nc.scalar.activation(vv[:, t % 2, :, 0:HD], ps[:, C:2 * C].rearrange("p (h e) -> p h e", h=NH),
                                         ACT.Copy).then_inc(free(key), 1)

            def attend(b):
                for i in range(TB):
                    key = ("oT", b, i)
                    ps = await_result(act_e, key)
                    if i >= 2:
                        await_computed(act_e, ("proj", b, i - 2))
                    nc.scalar.activation(oT[:, i % 2], ps[:, 0:C].rearrange("p (k n) -> p k n", k=KC),
                                         ACT.Copy).then_inc(free(key), 1)

            def turned(b):
                for g in range(NG):
                    for k in range(KC):
                        key = ("h2T", b, g, k)
                        ps = await_result(act_e, key)
                        nc.scalar.activation(h2T[:, b, k, g * W:(g + 1) * W], ps[:, :], ACT.Copy).then_inc(free(key), 1)
                key = ("router", b)
                ps = await_result(act_e, key)
                if b == 1:
                    act_e.wait_ge(recs_ready, 1)
                nc.scalar.activation(score, ps[:, 0:TB * E].rearrange("p (i e) -> p i e", i=TB),
                                     ACT.Sigmoid).then_inc(free(key), 1)

            def shared(b):
                for g in range(NG):
                    for m, (a, n) in enumerate(SC):
                        key = ("sg", b, g, m)
                        ps = await_result(act_e, key)
                        if (b, g) != (0, 0) and m == 0:
                            await_computed(act_e, ("sd", b, g * GT - 1) if g else ("sd", b - 1, TB - 1))
                        if (b, g, m) == (0, 0, 0):
                            act_e.wait_ge(lists_clear, 16)
                        nc.scalar.activation(sT[0:n, m, :], ps[0:n, :], ACT.Silu).then_inc(free(key), 1)

            head(0, 0)
            tiles(0, 0)
            head(0, 1)
            tiles(0, 1)
            attend(0)
            head(1, 0)
            turned(0)
            tiles(1, 0)
            head(1, 1)
            tiles(1, 1)
            attend(1)
            turned(1)
            shared(0)
            shared(1)

            def silu(c, n):
                act_e.wait_ge(gu_done, n + 1)
                if not isinstance(n, int) or n >= 2:
                    act_e.wait_ge(act_done, n - 1)
                nc.scalar.activation(act_g[:, c % 2, :], banks[1 + c % 2][:, 0:M], ACT.Silu).then_inc(silu_done, 1)

            def copy_act(c, n):
                act_e.wait_ge(act_turned, n + 1)
                wait(act_e, y_done, n - 1)
                nc.scalar.activation(aT[0:KD, c % 2, :, :], banks[3][0:KD, 0:2 * P].rearrange("p (m n) -> p m n", m=2),
                                     ACT.Copy).then_inc(aT_copied, 1)

            def weigh(c, n):
                act_e.wait_ge(y_done, n + 1)
                act_e.wait_ge(dest_listed, n + 1)
                nc.scalar.activation(yw[:, c, :], banks[4 + c % 2][:, 0:C], ACT.Copy,
                                     scale=pair_w[:, c:c + 1]).then_inc(y_scaled, 1)

            await_read(act_e, ("map",))
            silu(0, 0)

            def step(turn, last):
                for c in range(R):
                    n = R * turn + c
                    if not last or c + 1 < R:
                        silu(c + 1, n + 1)
                    copy_act(c, n)
                    if not first(n):
                        weigh((c - 1) % R, n - 1)
                    if last and c == R - 1:
                        weigh(c, n)

            blocks(act_e, step)

        @block.vector
        def _(dve):
            done = [0]

            def link(ins):
                done[0] += 1
                ins.then_inc(dve_own, 1)
                dve.wait_ge(dve_own, done[0])

            def link_free(ins, key):
                ins.then_inc(free(key), 1)
                await_read(dve, key)

            V = nc.vector
            await_read(dve, ("c",))
            V.tensor_copy(csB, csT.unsqueeze(3).broadcast_to([P, KC, B, P])).then_inc(cs_ready, 1)

            def first_norm(g):
                dve.wait_ge(ld_x[g], 16)
                for t in range(g * GT, (g + 1) * GT):
                    link(V.bn_stats(stats[:, t, :], X[:, t, :]))
                    V.bn_aggr(mv[:, t, :], stats[:, t, :]).then_inc(var_ready, 1)

            def normalise(g):
                dve.wait_ge(rstd_ready, g + 1)
                dve.wait_ge(var_ready, (g + 1) * GT)
                for t in range(g * GT, (g + 1) * GT):
                    V.tensor_scalar(xn[:, t, :], X[:, t, :], mv[:, t, 0:1], rstd[:, t:t + 1],
                                    ALU.subtract, ALU.mult).then_inc(xn_ready, 1)

            first_norm(0)
            ps = await_result(dve, ("modT",))
            link(V.tensor_copy(modT[:, 0:KC, :], ps[:, 0:KC * B].rearrange("p (k b) -> p k b", k=KC)))
            V.tensor_scalar(modT[:, KC:2 * KC, :], ps[:, KC * B:2 * KC * B].rearrange("p (k b) -> p k b", k=KC),
                            1.0, None, ALU.add).then_inc(free(("modT",)), 1)
            normalise(0)
            first_norm(1)
            normalise(1)
            for b in range(B):
                for s in range(2):
                    key = ("mod", b, s)
                    ps = await_result(dve, key)
                    gate = rows[:, b, 0, :] if s == 0 else gb[:, b, :]
                    src = ps[:, 0:C] if s == 0 else ps[:, C:2 * C]
                    other = ps[:, C:2 * C] if s == 0 else ps[:, 0:C]
                    link(V.tensor_scalar(rows[:, b, 3, :], src, -1.0, GUARD, ALU.mult, ALU.max))
                    link(V.tensor_tensor(rows[:, b, 3, :], src, rows[:, b, 3, :], ALU.max))
                    link(V.tensor_scalar(gate, src, 0.0, 2.0, ALU.is_ge, ALU.mult))
                    V.tensor_scalar(rows[:, b, 1 + s, :], other, float(s), None, ALU.add).then_inc(free(key), 1)
                    link(V.scalar_tensor_tensor(out=gate, in0=gate, scalar=-1.0, in1=rows[:, b, 3, :],
                                                op0=ALU.add, op1=ALU.mult))
            for k in range(KC):
                key = ("wpT", k)
                ps = await_result(dve, key)
                for b in range(B):
                    last = V.tensor_tensor(wpT[:, b, k, :], ps[:, 0:C], rows[:, b, 0, :], ALU.mult)
                last.then_inc(free(key), 1)
            dve.wait_ge(ld_proj, 32)
            link(V.tensor_tensor(bga[:, 1, :], bga[:, 0, :], rows[:, 1, 0, :], ALU.mult))
            V.tensor_tensor(bga[:, 0, :], bga[:, 0, :], rows[:, 0, 0, :], ALU.mult).then_inc(wpT_ready, 1)
            for g in range(2, NT // GT):
                first_norm(g)
            for g in range(2, NT // GT):
                normalise(g)

            def attend(b):
                for k in range(KC):
                    key = ("vk", b, k)
                    ps = await_result(dve, key)
                    if b == 0:
                        dve.wait_ge(consts, 10)
                    for h in range(HH):
                        r, c = slice(h * HD, (h + 1) * HD), slice(h * VE, (h + 1) * VE)
                        last = V.tensor_copy(nd[r, k, c], ps[r, c])
                    last.then_inc(free(key), 1)
                for i in range(TB + 3):
                    if i < TB:
                        normalise_heads(b, i)
                    if i >= 3:
                        residual(b, i - 3)
                        if (i - 3) % GT == GT - 1:
                            second_norm(b, (i - 3) // GT)

            def normalise_heads(b, i):
                key = ("o", b, i)
                ps = await_result(dve, key)
                heads = ps[:, 0:NH * VE].rearrange("p (h e) -> p h e", h=NH)
                link(V.tensor_scalar(rden[:, i % 2, :], heads[:, :, HD], DIV_EPS, None, ALU.add))
                link(V.reciprocal(rden[:, i % 2, :], rden[:, i % 2, :]))
                if i >= 2:
                    await_computed(dve, ("oT", b, i - 2))
                V.tensor_tensor(o[:, i % 2, :].rearrange("p (h e) -> p h e", h=NH), heads[:, :, 0:HD],
                                rden[:, i % 2, :].unsqueeze(2).broadcast_to([P, NH, HD]), ALU.mult).then_inc(free(key), 1)

            def residual(b, i):
                t = b * TB + i
                key = ("proj", b, i)
                ps = await_result(dve, key)
                dve.wait_ge(xb_ready, t + 1)
                link_free(V.tensor_tensor(X[:, t, :], ps[:, 0:C], X[:, t, :], ALU.add), key)
                link(V.bn_stats(stats[:, t, :], X[:, t, :]))
                V.bn_aggr(mv2[:, t, :], stats[:, t, :]).then_inc(var2_ready, 1)

            def second_norm(b, g):
                if b == 0 and g == 0:
                    dve.wait_ge(sums_clear, 32)
                dve.wait_ge(rstd2_ready, b * NG + g + 1)
                dve.wait_ge(var2_ready, b * TB + (g + 1) * GT)
                if b == 1 and g == 0:
                    dve.wait_ge(h2_stored, 16 * NG)
                    await_computed(dve, ("h2T", 0, NG - 1, KC - 1))
                for i in range(g * GT, (g + 1) * GT):
                    t = b * TB + i
                    last = V.scalar_tensor_tensor(out=h2[:, i, :], in0=X[:, t, :], scalar=mv2[:, t, 0:1],
                                                  in1=rows[:, b, 2, :], op0=ALU.subtract, op1=ALU.mult)
                link(last)
                for i in range(g * GT, (g + 1) * GT):
                    t = b * TB + i
                    V.scalar_tensor_tensor(out=h2[:, i, :], in0=h2[:, i, :], scalar=rstd2[:, t:t + 1],
                                           in1=rows[:, b, 1, :], op0=ALU.mult, op1=ALU.add).then_inc(h2_ready, 1)

            def over(ap, shape, axis):
                return ap.unsqueeze(axis).broadcast_to(shape)

            def choose(b):
                shape = [P, TB, E]
                key = ("router", b)
                await_read(dve, key)
                if b == 0:
                    dve.wait_ge(ld_route, 32)
                link(V.tensor_tensor(sfc, score, over(bias_bc[:, :], shape, 1), ALU.add))
                q = sfc.rearrange("p i (g j) -> p (i g) j", j=EG)
                flat = [pair[:, a].rearrange("p i g -> p (i g)") for a in range(4)]
                link(V.tensor_tensor(flat[0], q[:, :, 0], q[:, :, 1], ALU.max))
                link(V.tensor_tensor(flat[1], q[:, :, 0], q[:, :, 1], ALU.min))
                link(V.tensor_tensor(flat[2], q[:, :, 2], q[:, :, 3], ALU.max))
                link(V.tensor_tensor(flat[3], q[:, :, 2], q[:, :, 3], ALU.min))
                g_flat = gs.rearrange("p i g -> p (i g)")
                link(V.tensor_tensor(g_flat, flat[0], flat[2], ALU.add))
                link(V.tensor_tensor(flat[1], flat[0], flat[1], ALU.add))
                link(V.tensor_tensor(flat[3], flat[2], flat[3], ALU.add))
                link(V.tensor_tensor(flat[1], flat[1], flat[3], ALU.max))
                link(V.tensor_tensor(g_flat, g_flat, flat[1], ALU.max))

                def largest(values, n, width):
                    for i in range(TB):
                        last = V.max(top[:, i, :], values[:, i, :])
                    link(last)
                    for i in range(TB):
                        last = V.max_index(top_i[:, i, :], top[:, i, :], values[:, i, :])
                    link(last)
                    link(V.tensor_copy(top_f, top_i[:, :, :]))
                    one = chosen[:, :, 0:n, 0:width]
                    s4 = [P, TB, n, width]
                    link(V.tensor_tensor(one, iota_e[:, 0:width].unsqueeze(1).unsqueeze(1).broadcast_to(s4),
                                         top_f[:, :, 0:n].unsqueeze(3).broadcast_to(s4), ALU.is_equal))
                    return one

                if b == 0:
                    dve.wait_ge(consts, 10)
                one = largest(gs, TOPG, G)
                link(V.tensor_reduce(gmask[:, 0], one.rearrange("p i k g -> p i g k"), AX.X, ALU.add))
                link(V.tensor_scalar(gmask[:, 1], gmask[:, 0], -1.0, -LOW, ALU.add, ALU.mult))
                m_q = sel.rearrange("p i (g j) -> p (i g) j", j=EG)
                s3 = [P, TB * G, EG]
                link(V.tensor_tensor(m_q, q, gmask[:, 0].rearrange("p i g -> p (i g)").unsqueeze(2).broadcast_to(s3), ALU.mult))
                link(V.tensor_tensor(m_q, m_q, gmask[:, 1].rearrange("p i g -> p (i g)").unsqueeze(2).broadcast_to(s3), ALU.add))
                one = largest(sel, TOPK, E)
                link(V.tensor_reduce(sel, one.rearrange("p i k e -> p i e k"), AX.X, ALU.add))
                if b == 1:
                    await_computed(dve, ("ranks", 0))
                V.tensor_copy(sel_bf, sel).then_inc(sel_ready, 1)
                s4 = [P, TB, TOPK, E]
                link(V.tensor_tensor(weighed, one, over(score, s4, 2), ALU.mult))
                link(V.tensor_reduce(recs[:, b * TB:(b + 1) * TB, :, 2], weighed, AX.X, ALU.add))

            def place(b):
                key = ("ranks", b)
                ps = await_result(dve, key)
                for i in range(TB):
                    link(V.tensor_tensor(rank[:, i, :], ps[:, i * E:(i + 1) * E], used[:, :], ALU.add))
                    ins = V.tensor_tensor(used[:, :], ps[:, (TB + i) * E:(TB + i + 1) * E], used[:, :], ALU.add)
                    if i < TB - 1:
                        link(ins)
                    else:
                        link_free(ins, key)
                link(V.tensor_copy(rank_i[:, 0], rank))
                link(V.tensor_scalar(rank_i[:, 1], rank_i[:, 0], 7, None, ALU.arith_shift_right))
                link(V.tensor_scalar(rank_i[:, 0], rank_i[:, 0], P - 1, None, ALU.bitwise_and))
                link(V.tensor_scalar(rank, rank_i[:, 0], float(NCOL), None, ALU.mult))
                link(V.tensor_tensor(rank, rank, rank_i[:, 1], ALU.add))
                link(V.scalar_tensor_tensor(out=rank, in0=over(iota_e[:, :], [P, TB, E], 1), scalar=float(NT), in1=rank,
                                            op0=ALU.mult, op1=ALU.add))
                s4 = [P, TB, TOPK, E]
                link(V.tensor_tensor(weighed, chosen, over(rank, s4, 2), ALU.mult))
                link(V.tensor_reduce(top_f[:, :, 0:TOPK], weighed, AX.X, ALU.add))
                V.tensor_copy(rows_i[:, b * TB:(b + 1) * TB, :], top_f[:, :, 0:TOPK]).then_inc(recs_ready, 1)

            def shared(b):
                for g in range(NG):
                    for m, (a, n) in enumerate(SC):
                        key = ("su", b, g, m)
                        ps = await_result(dve, key)
                        await_read(dve, ("sg", b, g, m))
                        V.tensor_tensor(sT[0:n, m, :], sT[0:n, m, :], ps[0:n, :], ALU.mult).then_inc(free(key), 1)
                    for i in range(g * GT, (g + 1) * GT):
                        t = b * TB + i
                        key = ("sd", b, i)
                        ps = await_result(dve, key)
                        link_free(V.tensor_tensor(sh_tmp, ps[:, 0:C], gb[:, b, :], ALU.mult), key)
                        V.tensor_tensor(X[:, t, :], X[:, t, :], sh_tmp, ALU.add).then_inc(base_ready, 1)
                        dve.wait_ge(base_ready, t + 1)

            attend(0)
            choose(0)
            place(0)
            attend(1)
            choose(1)
            place(1)

            shape = [P, E, NT]
            link(V.tensor_tensor(more, used[:, :].unsqueeze(2).broadcast_to(shape),
                                 iota_n[:, :].unsqueeze(1).broadcast_to(shape), ALU.is_gt))
            link(V.tensor_reduce(seg[:, 0, :], more, AX.X, ALU.add))
            link(V.memset(seg[:, 2, :], 1.0))
            link(V.tensor_tensor_scan(seg[:, 1, :], seg[:, 2, :], seg[:, 0, :], 0.0, ALU.mult, ALU.add))
            link(V.tensor_tensor(seg[:, 0, :], seg[:, 1, :], seg[:, 0, :], ALU.subtract))
            link(V.tensor_scalar(seg[:, 2, :], seg[:, 1, :], iota_p[:, 0:1], None, ALU.is_le))
            link(V.tensor_reduce(mapf[:, 0:1], seg[:, 2, :], AX.X, ALU.add))
            link(V.tensor_scalar(mapf[:, 0:1], mapf[:, 0:1], float(E - 1), None, ALU.min))
            link(V.tensor_scalar(seg[:, 3, :], iota_e[:, :], mapf[:, 0:1], None, ALU.is_equal))
            link(V.scalar_tensor_tensor(out=seg[:, 0, :], in0=iota_e[:, :], scalar=float(NT), in1=seg[:, 0, :],
                                        op0=ALU.mult, op1=ALU.subtract))
            link(V.tensor_tensor(seg[:, 3, :], seg[:, 3, :], seg[:, 0, :], ALU.mult))
            link(V.tensor_reduce(mapf[:, 1:2], seg[:, 3, :], AX.X, ALU.add))
            link(V.tensor_tensor(mapf[:, 1:2], mapf[:, 1:2], iota_p[:, 0:1], ALU.add))
            link(V.tensor_tensor(mapf[:, 2:3], iota_p[:, 0:1], seg[:, 1, E - 1:E], ALU.is_ge))
            link(V.scalar_tensor_tensor(out=mapf[:, 1:2], in0=mapf[:, 2:3], scalar=2.0 * P * NT, in1=mapf[:, 1:2],
                                        op0=ALU.mult, op1=ALU.add))
            link(V.tensor_scalar(mapf[:, 1:2], mapf[:, 1:2], float(EMPTY), None, ALU.min))
            link(V.tensor_scalar(seg[:, 3, 0:TURNS], iota_e[:, 0:TURNS], float(R), None, ALU.mult))
            link(V.tensor_scalar(seg[:, 3, 0:TURNS], seg[:, 3, 0:TURNS], seg[:, 1, E - 1:E], None, ALU.is_lt))
            link(V.tensor_reduce(mapf[:, 2:3], seg[:, 3, 0:TURNS], AX.X, ALU.add))
            V.tensor_scalar(mapf[:, 2:3], mapf[:, 2:3], -2.0, None, ALU.add).then_inc(mapf_ready, 1)
            dve.wait_ge(mapf_ready, 1)
            shared(0)
            shared(1)
            await_computed(dve, ("map",))
            link(V.memset(map_i, 0))
            link(V.tensor_copy(map_i[0:1, 2 * MAP_W:2 * MAP_W + 1], mapf[0:1, 2:3]))
            ps = await_result(dve, ("map",))
            V.tensor_copy(map_i[0:1, 0:2 * MAP_W].rearrange("p (a n) -> p a n", a=2)[:, :, 1:P + 1],
                          ps[0:1, 0:2 * P].rearrange("p (a n) -> p a n", a=2)).then_inc(free(("map",)), 1)
            await_read(dve, ("map",))
            dve.wait_ge(ld_lists, 16)

            def tokens(c, col, turn):
                if not isinstance(turn, int) or turn > 0:
                    dve.wait_ge(gathered[c], 16 * turn)
                V.tensor_copy(tok_i[:, c:c + 1], lists_sb[:, bass.ds(col * 4, 1)]).then_inc(tok_listed, 1)

            def dests(c, col, turn):
                if not isinstance(turn, int) or turn > 0:
                    dve.wait_ge(scattered[c], 16 * turn)
                V.tensor_copy(dest_i[:, c:c + 1], lists_sb[:, bass.ds(col * 4 + 1, 1)])
                V.tensor_copy(pair_w[:, c:c + 1], lists_sb[:, bass.ds(col * 4 + 2, 1)]).then_inc(dest_listed, 1)

            def copy_x(c, n):
                dve.wait_ge(x_turned, n + 1)
                if not isinstance(n, int) or n >= 2:
                    dve.wait_ge(gu_done, n - 1)
                V.tensor_copy(xT[:, c % 2], banks[0][:, 0:C].rearrange("p (k n) -> p k n", k=KC)).then_inc(xT_copied, 1)

            def multiply(c, n):
                dve.wait_ge(silu_done, n + 1)
                if not isinstance(n, int) or n >= 2:
                    dve.wait_ge(act_turned, n - 1)
                V.tensor_tensor(act[:, c % 2, :], act_g[:, c % 2, :], banks[1 + c % 2][:, M:M2], ALU.mult).then_inc(act_done, 1)

            DVE = mybir.EngineType.DVE
            cols = load_values(dve, DVE, 1, 0, 0)
            for c in range(R):
                tokens(c, cols[c], 0)
            for c in range(2):
                copy_x(c, c)
            multiply(0, 0)

            def step(turn, last):
                cols = load_values(dve, DVE, 1, turn, 0)
                for c in range(R):
                    n = R * turn + c
                    if not last or c + 2 < R:
                        copy_x(c, n + 2)
                    if not last or c + 1 < R:
                        multiply(c + 1, n + 1)
                    if not last:
                        tokens(c, cols[c + R], turn + 1)
                    dests(c, cols[c], turn)

            blocks(dve, step)

            for g in range(NT // GT):
                dve.wait_ge(fetched[g], 32)
                rows_g = slice(g * GT, (g + 1) * GT)
                link(V.tensor_tensor(sums[:, 0, rows_g, :], sums[:, 0, rows_g, :], sums[:, 1, rows_g, :], ALU.add))
                link(V.tensor_tensor(sums[:, 0, rows_g, :], sums[:, 0, rows_g, :],
                                     over(gb[:, g // NG, :], [P, GT, C], 1), ALU.mult))
                V.tensor_tensor(X[:, rows_g, :], X[:, rows_g, :], sums[:, 0, rows_g, :], ALU.add).then_inc(out_ready, 1)

        @block.tensor
        def _(pe):
            mm = nc.tensor.matmul

            def turn(out_ap, in_ap):
                return nc.tensor.transpose(out_ap, in_ap, ident[:, :])

            pe.wait_ge(consts, 10)
            pe.wait_ge(ld_c, 16)
            ps = fill(pe, ("c",))
            for k in range(KC):
                last = nc.tensor.transpose(ps[:, k * B:(k + 1) * B], c_row[:, k * P:(k + 1) * P], ident[0:B, 0:B])
            last.then_inc(full(("c",)), 1)
            pe.wait_ge(ld_qkv, 16)
            for g in range(2 * KC):
                ps = fill(pe, ("wT", g))
                for o3 in range(3):
                    last = turn(ps[:, o3 * P:(o3 + 1) * P], wqkv_raw[:, (g % 2) * 3 + o3, (g // 2) * P:(g // 2 + 1) * P])
                last.then_inc(full(("wT", g)), 1)
            pe.wait_ge(ld_mod, 16)
            await_read(pe, ("c",))
            ps = fill(pe, ("modT",))
            for j in range(2 * KC):
                for k in range(KC):
                    last = mm(ps[:, j * B:(j + 1) * B], wmod_sb[:, k, j * P:(j + 1) * P], csT[:, k, :],
                              start=k == 0, stop=k == KC - 1)
            last.then_inc(full(("modT",)), 1)

            def modulation():
                pe.wait_ge(cs_ready, 1)
                for b in range(B):
                    for s in range(2):
                        ps = fill(pe, ("mod", b, s))
                        for k in range(KC):
                            a = 2 * C + s * 2 * C
                            last = mm(ps[:, :], csB[:, k, b, :], wmod_sb[:, k, a:a + 2 * C], start=k == 0, stop=k == KC - 1)
                        last.then_inc(full(("mod", b, s)), 1)
                pe.wait_ge(ld_proj, 32)
                for k in range(KC):
                    ps = fill(pe, ("wpT", k))
                    for j in range(KC):
                        last = turn(ps[:, j * P:(j + 1) * P], wproj_raw[:, j, k * P:(k + 1) * P])
                    last.then_inc(full(("wpT", k)), 1)

            def drained_by(key):
                await_read(pe, key)

            def outer(b, i):
                t = b * TB + i
                drained_by(("kv", b, i))
                for k in range(KC):
                    if i == 0:
                        wait(pe, drained[6 + k], use[("vk", b, k)][1] - 1)
                    last = mm(of(("vk", b, k))[:, 0:HH * VE], kk[:, t % 2, k * P:(k + 1) * P],
                              vv[:, t % 2, k * HH:(k + 1) * HH, :], start=i == 0, stop=i == TB - 1)
                    if i == TB - 1:
                        last.then_inc(full(("vk", b, k)), 1)
                if i < TB - 1:
                    last.then_inc(kv_used, 1)

            def head(b, g):
                keys = [("hT", b, g, k) for k in range(KC)]
                for k in range(KC):
                    fill(pe, keys[k])
                for i in range(GT):
                    t = b * TB + g * GT + i
                    pe.wait_ge(xn_ready, t + 1)
                    for k in range(KC):
                        last = turn(of(keys[k])[:, i * P:(i + 1) * P], xn[:, t, k * P:(k + 1) * P])
                        if i == GT - 1:
                            last.then_inc(full(keys[k]), 1)
                for k in range(KC):
                    drained_by(keys[k])
                for m in range(KC):
                    key = ("q", b, g, m)
                    ps = fill(pe, key)
                    if b == 0 and g == 0 and m == 0:
                        drained_by(("wT", 2 * KC - 1))
                        drained_by(("wT", 2 * KC - 2))
                    for k in range(KC):
                        last = mm(ps[:, :], wT[:, k, m * P:(m + 1) * P], hT[:, k, :], start=k == 0, stop=k == KC - 1)
                    last.then_inc(full(key), 1)

            def tiles(b, g):
                for i in range(g * GT, (g + 1) * GT):
                    key = ("kv", b, i)
                    ps = fill(pe, key)
                    a = (i % GT) * P
                    for k in range(KC):
                        last = mm(ps[:, :], hT[:, k, a:a + P], wT[:, k, C:3 * C], start=k == 0, stop=k == KC - 1)
                    last.then_inc(full(key), 1)
                    if i > g * GT:
                        outer(b, i - 1)
                outer(b, (g + 1) * GT - 1)

            def attend(b):
                for k in range(KC):
                    drained_by(("vk", b, k))
                if b == 0:
                    pe.wait_ge(wpT_ready, 1)
                drained_by(("q", b, NG - 1, KC - 1))
                for i in range(TB + 2):
                    if i < TB:
                        key = ("o", b, i)
                        ps = fill(pe, key)
                        for k in range(KC):
                            last = mm(ps[:, k * HH * VE:(k + 1) * HH * VE], qT[:, k, i * P:(i + 1) * P], nd[:, k, :],
                                      start=True, stop=True)
                        last.then_inc(full(key), 1)
                    if 1 <= i <= TB:
                        key = ("oT", b, i - 1)
                        drained_by(("o", b, i - 1))
                        ps = fill(pe, key)
                        for k in range(KC):
                            last = turn(ps[:, k * P:(k + 1) * P], o[:, (i - 1) % 2, k * P:(k + 1) * P])
                        last.then_inc(full(key), 1)
                    if i >= 2:
                        key = ("proj", b, i - 2)
                        drained_by(("oT", b, i - 2))
                        ps = fill(pe, key)
                        for k in range(KC):
                            last = mm(ps[:, 0:C], oT[:, i % 2, k, :], wpT[:, b, k, :], start=k == 0, stop=k == KC - 1)
                        last.then_inc(full(key), 1)

            def turn_h2(b):
                for g in range(NG):
                    keys = [("h2T", b, g, k) for k in range(KC)]
                    for k in range(KC):
                        fill(pe, keys[k])
                    for i in range(GT):
                        pe.wait_ge(h2_ready, b * TB + g * GT + i + 1)
                        for k in range(KC):
                            last = turn(of(keys[k])[:, i * P:(i + 1) * P], h2[:, g * GT + i, k * P:(k + 1) * P])
                            if i == GT - 1:
                                last.then_inc(full(keys[k]), 1)
                if b == 0:
                    pe.wait_ge(ld_route, 32)
                key = ("router", b)
                ps = fill(pe, key)
                for g in range(NG):
                    for k in range(KC):
                        drained_by(("h2T", b, g, k))
                    for i in range(g * GT, (g + 1) * GT):
                        for k in range(KC):
                            last = mm(ps[:, i * E:(i + 1) * E], h2T[:, b, k, i * P:(i + 1) * P], router[:, k, :],
                                      start=k == 0, stop=k == KC - 1)
                last.then_inc(full(key), 1)

            def ranks(b):
                pe.wait_ge(sel_ready, b + 1)
                ps = fill(pe, ("ranks", b))
                w = TB * E
                moving = sel_bf.rearrange("p i e -> p (i e)")
                mm(ps[:, 0:w], tri[:, :], moving, start=True, stop=True)
                mm(ps[:, w:2 * w], ones_bf[:, :], moving, start=True, stop=True).then_inc(full(("ranks", b)), 1)

            def shared(b):
                if b == 0:
                    pe.wait_ge(ld_sh, 16 * (2 + len(SC)))
                for g in range(NG):
                    for m, (a, n) in enumerate(SC):
                        for s, name in enumerate(("sg", "su")):
                            key = (name, b, g, m)
                            ps = fill(pe, key)
                            for k in range(KC):
                                last = mm(ps[0:n, :], sh_gu[:, s, k, a:a + n], h2T[:, b, k, g * W:(g + 1) * W],
                                          start=k == 0, stop=k == KC - 1)
                            last.then_inc(full(key), 1)
                    for m in range(len(SC)):
                        drained_by(("su", b, g, m))
                    for i in range(GT):
                        key = ("sd", b, g * GT + i)
                        ps = fill(pe, key)
                        for m, (a, n) in enumerate(SC):
                            last = mm(ps[:, 0:C], sT[0:n, m, i * P:(i + 1) * P], sh_dn[0:n, m, :],
                                      start=m == 0, stop=m == len(SC) - 1)
                        last.then_inc(full(key), 1)

            head(0, 0)
            tiles(0, 0)
            modulation()
            head(0, 1)
            tiles(0, 1)
            attend(0)
            head(1, 0)
            turn_h2(0)
            tiles(1, 0)
            head(1, 1)
            ranks(0)
            tiles(1, 1)
            attend(1)
            turn_h2(1)
            ranks(1)
            shared(0)
            shared(1)
            pe.wait_ge(mapf_ready, 1)
            ps = fill(pe, ("map",))
            for a in range(2):
                last = mm(ps[0:1, a * P:(a + 1) * P], mapf[:, a:a + 1], ident[:, :], start=True, stop=True)
            last.then_inc(full(("map",)), 1)

            for bank in range(8):
                pe.wait_ge(drained[bank], uses[bank])
            pe.wait_ge(ld_early, 16 * EARLY // 8 * 2 * KC)
            pe.wait_ge(ld_late, 16 * (2 + 2 * KC))

            def turn_x(s, n, turn):
                pe.wait_ge(gathered[s], 16 * (turn + 1))
                wait(pe, xT_copied, n)
                for k in range(KC):
                    last = nc.tensor.transpose(banks[0][:, k * P:(k + 1) * P], xg[:, s, k * P:(k + 1) * P], ident[:, :])
                last.then_inc(x_turned, 1)

            def gate_and_up(c, n, e):
                pe.wait_ge(xT_copied, n + 1)
                for k in range(KC):
                    last = mm(banks[1 + c % 2][:, 0:M2], xT[:, c % 2, k, :],
                              gate_up[:, bass.ds(e * (KC * M2) + k * M2, M2)], start=k == 0, stop=k == KC - 1)
                last.then_inc(gu_done, 1)

            def turn_act(c, n):
                pe.wait_ge(act_done, n + 1)
                wait(pe, aT_copied, n)
                for m in range(2):
                    last = nc.tensor.transpose(banks[3][0:KD, m * P:(m + 1) * P], act[:, c % 2, m * KD:(m + 1) * KD], ident[:, :])
                last.then_inc(act_turned, 1)

            def down_rows(c, n, e):
                pe.wait_ge(aT_copied, n + 1)
                wait(pe, y_scaled, n - 1)
                for m in range(2):
                    last = mm(banks[4 + c % 2][:, 0:C], aT[0:KD, c % 2, m, :],
                              down[0:KD, bass.ds(e * C + m * E * C, C)], start=m == 0, stop=m == 1)
                last.then_inc(y_done, 1)

            PE = mybir.EngineType.PE
            experts = load_values(pe, PE, 0, 0, 0)
            for c in range(2):
                turn_x(c, c, 0)
            for c in range(2):
                gate_and_up(c, c, experts[c])

            def step(turn, last):
                experts = load_values(pe, PE, 0, turn, -1)
                for c in range(R):
                    n = R * turn + c
                    if not last or c + 2 < R:
                        turn_x((c + 2) % R, n + 2, turn + (c + 2) // R)
                    turn_act(c, n)
                    if not first(n):
                        down_rows((c - 1) % R, n - 1, experts[c])
                    if not last or c + 2 < R:
                        gate_and_up(c, n + 2, experts[c + 3])
                    if last and c == R - 1:
                        down_rows(c, n, experts[c + 1])

            blocks(pe, step)


_INS = ['L0_attn_x', 'L0_attn_w_qkv', 'L0_attn_w_proj', 'L0_attn_b_proj', 'L0_ffn_w_router', 'L0_ffn_corr_bias',
        'L0_ffn_gate_w', 'L0_ffn_up_w', 'L0_ffn_down_w', 'L0_ffn_sh_gate_w', 'L0_ffn_sh_up_w', 'L0_ffn_sh_down_w',
        'L0_c', 'L0_wmod']


def kernel(**inputs):
    import numpy as _np
    import concourse.bacc as _bacc
    from concourse import mybir as _mybir
    from concourse.bass_utils import run_bass_kernel_spmd as _run

    nc = _bacc.Bacc("TRN2", target_bir_lowering=False, num_devices=1)
    arrays, args = {}, []
    for name in _INS:
        a = _np.ascontiguousarray(inputs[name])
        arrays[f"in_{name}"] = a
        args.append(nc.dram_tensor(f"in_{name}", a.shape, _mybir.dt.from_np(a.dtype), kind="ExternalInput").ap())
    shape = inputs["L0_attn_x"].shape
    args.append(nc.dram_tensor("out_0", shape, _mybir.dt.float32, kind="ExternalOutput").ap())
    build_block(nc, *args)
    r = _run(nc, [arrays], core_ids=[0])
    return r.results[0]["out_0"]
```

```python
def build_block(nc, x_in, w_qkv, w_proj, b_proj, w_router, corr_bias, gate_w, up_w, down_w,
                sh_gate_w, sh_up_w, sh_down_w, cond, w_mod, out):
    import concourse.bass as bass
    from concourse import mybir
    from contextlib import ExitStack

    f32, i32, u32, bf16 = mybir.dt.float32, mybir.dt.int32, mybir.dt.uint32, mybir.dt.bfloat16
    ALU, ACT, AX = mybir.AluOpType, mybir.ActivationFunctionType, mybir.AxisListType

    P = 128
    B, N, C = x_in.shape
    T = B * N
    NT = T // P
    TB = NT // B
    GT = 4
    NG = TB // GT
    W = GT * P
    KC = C // P
    HD = 32
    NH = C // HD
    HH = NH // KC
    VE = HD + 1
    E, _, M = gate_w.shape
    M2 = 2 * M
    KD = M // 2
    SM = sh_gate_w.shape[1]
    SC = [(a, min(P, SM - a)) for a in range(0, SM, P)]
    TOPK, G, TOPG = 6, 8, 4
    EG = E // G
    NBLK = (T * TOPK - E) // P + E + 1
    TURNS = -(-NBLK // 4)
    FEWEST = T * TOPK // P // 4 - 1
    MAP_W = P + 8
    NCOL = E * NT + 1
    EMPTY = NCOL - 1
    LN_EPS, DIV_EPS, GUARD = 1e-5, 1e-15, 0.25
    LOW = -1.5e38

    x_v = x_in.rearrange("b (p i) c -> p b i c", p=P)
    out_v = out.rearrange("b (p i) c -> p b i c", p=P)

    ctx = ExitStack()
    with ctx:
        def sb(name, shape, dt=f32):
            return ctx.enter_context(nc.sbuf_tensor(name, shape, dt))

        def sem(name):
            return ctx.enter_context(nc.semaphore(name))

        def shared_part(region, width):
            at = [0]

            def take(n):
                a = at[0]
                at[0] += n
                assert at[0] <= width, (at[0], width)
                return region[:, a:a + n]
            return take

        h2_dram = nc.dram_tensor("h2_rows", (T, C), f32).ap()
        lists = nc.dram_tensor("pair_lists", (NCOL * P, 4), f32).ap()
        token_sums = [nc.dram_tensor(f"token_sums{a}", (T, C), f32).ap() for a in range(2)]
        h2_tiles = h2_dram.rearrange("(b p i) c -> p b i c", b=B, p=P)
        sums_v = [a.rearrange("(b p i) c -> p b i c", b=B, p=P) for a in token_sums]

        EARLY = 24
        gate_up = sb("gate_up", [P, E * KC * M2])
        gu_v = gate_up[:, :].rearrange("p (e k m) -> p e k m", e=E, k=KC)
        down = sb("down", [P, 2 * E * C])
        dn_v = down[:, :].rearrange("p (m f) -> p m f", m=2)
        X = sb("X", [P, NT, C])
        tok_buf = sb("tok_buf", [P, NT * C])
        xn = tok_buf[:, :].rearrange("p (i c) -> p i c", i=NT)
        h2T = tok_buf[:, :].rearrange("p (b k n) -> p b k n", b=B, k=KC)
        sh_gu = sb("sh_gu", [P, 2, KC, SM])
        sh_dn = sb("sh_dn", [P, len(SC), C])
        router = sb("router", [P, KC, E])
        bias_bc = sb("bias_bc", [P, E])
        gb = sb("gb", [P, B, C])
        sT = sb("sT", [P, len(SC), W])
        sh_tmp = sb("sh_tmp", [P, C])
        recs = sb("recs", [P, NT, TOPK, 4])
        rows_i = sb("rows_i", [P, NT, TOPK], i32)
        ident = sb("ident", [P, P])
        tri = sb("tri", [P, P], bf16)
        ones_bf = sb("ones_bf", [P, P], bf16)
        iota_e = sb("iota_e", [P, E])
        iota_p = sb("iota_p", [P, 1])
        sigmoid_table = sb("sigmoid_table", [P, 1])
        used = sb("used", [P, E])
        stats = sb("stats", [P, NT, 6])
        mv = sb("mv", [P, NT, 2])
        mv2 = sb("mv2", [P, NT, 2])
        rstd = sb("rstd", [P, NT])
        rstd2 = sb("rstd2", [P, NT])
        minus_half = sb("minus_half", [P, TB])
        modT = sb("modT", [P, 4, B])
        mapf = sb("mapf", [P, 4])
        iota_n = sb("iota_n", [P, NT])
        later = sb("later", [P, E, TB])

        part = shared_part(down, 2 * E * C)
        wmod_sb = part(KC * 6 * C).rearrange("p (k n) -> p k n", k=KC)
        c_row = part(C)[0:B, :]
        csT = part(KC * B).rearrange("p (k b) -> p k b", k=KC)
        csB = part(KC * B * P).rearrange("p (k b n) -> p k b n", k=KC, b=B)
        wqkv_raw = part(3 * KC * C).rearrange("p (o c) -> p o c", o=3 * KC)
        wproj_raw = part(KC * C).rearrange("p (o c) -> p o c", o=KC)
        wT = part(KC * 3 * C).rearrange("p (k o) -> p k o", k=KC)
        wpT = part(B * KC * C).rearrange("p (b k o) -> p b k o", b=B, k=KC)
        rows = part(B * 4 * C).rearrange("p (b r c) -> p b r c", b=B, r=4)
        bga = part(B * C).rearrange("p (b c) -> p b c", b=B)
        hT = part(KC * W).rearrange("p (k n) -> p k n", k=KC)
        qT = part(KC * N).rearrange("p (k n) -> p k n", k=KC)
        kk = part(2 * C).rearrange("p (s c) -> p s c", s=2)
        vv = part(2 * NH * VE).rearrange("p (s h e) -> p s h e", s=2, h=NH)
        nd = part(KC * HH * VE).rearrange("p (k n) -> p k n", k=KC)
        rden = part(2 * NH).rearrange("p (s h) -> p s h", s=2)
        o = wqkv_raw[:, 0:2, :]
        oT = part(2 * KC * P).rearrange("p (s k n) -> p s k n", s=2, k=KC)

        part = shared_part(gate_up[:, EARLY * KC * M2:], (E - EARLY) * KC * M2)
        h2 = part(TB * C).rearrange("p (i c) -> p i c", i=TB)
        empties = gate_up[:, EARLY * KC * M2 + TB * C:EARLY * KC * M2 + TB * C + NCOL * 4]
        chosen = part(TB * TOPK * E // 2).bitcast(bf16).rearrange("p (i k e) -> p i k e", i=TB, k=TOPK)
        score = part(TB * E).rearrange("p (i e) -> p i e", i=TB)
        sfc = part(TB * E).rearrange("p (i e) -> p i e", i=TB)
        sel = part(TB * E).rearrange("p (i e) -> p i e", i=TB)
        rank = part(TB * E).rearrange("p (i e) -> p i e", i=TB)
        tmp = wmod_sb[:, :, :].rearrange("p k n -> p (k n)")
        weighed = tmp[:, 0:TB * TOPK * E].rearrange("p (i k e) -> p i k e", i=TB, k=TOPK)
        at = TB * TOPK * E
        before = tmp[:, at:at + TB * E].rearrange("p (e i) -> p e i", i=TB)
        at += TB * E
        pair = tmp[:, at:at + 4 * TB * G].rearrange("p (a m h) -> p a m h", a=2, h=2)
        at += 4 * TB * G
        gs = tmp[:, at:at + TB * G].rearrange("p (i g) -> p i g", i=TB)
        at += TB * G
        gmask = tmp[:, at:at + TB * G].rearrange("p (i g) -> p i g", i=TB)
        at += TB * G
        top = tmp[:, at:at + TB * 8].rearrange("p (i k) -> p i k", i=TB)
        at += TB * 8
        top_f = tmp[:, at:at + TB * 8].rearrange("p (i k) -> p i k", i=TB)
        at += TB * 8
        top_i = tmp[:, at:at + TB * 8].bitcast(u32).rearrange("p (i k) -> p i k", i=TB)
        at += TB * 8
        assert at <= KC * 6 * C

        part = shared_part(tok_buf, NT * C // 2)
        R = 4
        xg = part(R * C).rearrange("p (s c) -> p s c", s=R)
        xT = part(2 * C).rearrange("p (s k n) -> p s k n", s=2, k=KC)
        aT = part(2 * 2 * P).rearrange("p (s m n) -> p s m n", s=2, m=2)
        part = shared_part(tok_buf[:, NT * C // 2:], NT * C // 2)
        yw = part(R * C).rearrange("p (s c) -> p s c", s=R)
        act_g = part(2 * M).rearrange("p (s m) -> p s m", s=2)
        act = part(2 * M).rearrange("p (s m) -> p s m", s=2)
        map_i = down[96:97, 0:2 * MAP_W + 1].bitcast(i32)
        assert KD <= 96
        more = tmp[:, 0:E * NT].rearrange("p (e n) -> p e n", e=E)
        seg = tmp[:, E * NT:(NT + 4) * E].rearrange("p (a e) -> p a e", a=4)
        tok_rec = sb("tok_rec", [P, R, 4])
        dest_rec = sb("dest_rec", [P, R, 4])
        sums = gate_up[:, 0:2 * NT * C].rearrange("p (a i c) -> p a i c", a=2, i=NT)

        banks = [ctx.enter_context(nc.psum_tensor(f"bank{i}", [P, 512], f32)) for i in range(8)]

        filled = [sem(f"bank{i}_filled") for i in range(8)]
        drained = [sem(f"bank{i}_drained") for i in range(8)]
        ld_c, ld_mod, ld_qkv, ld_proj, ld_route, ld_sh = (sem("ld_" + n) for n in ("c", "mod", "qkv", "proj", "route", "shared"))
        ld_mod_rows = sem("ld_mod_rows")
        ld_x = [sem(f"ld_x{i}") for i in range(NT // GT)]
        ld_early, ld_late = sem("ld_early_weights"), sem("ld_late_weights")
        consts, ident_ready = sem("constants_ready"), sem("identity_ready")
        pool_passed = sem("pool_passed_waits")
        dve_own, pool_own = sem("dve_own_steps"), sem("pool_own_steps")
        var_ready, rstd_ready, xn_ready, xb_ready = (sem(n) for n in ("var_ready", "rstd_ready", "xn_ready", "xb_ready"))
        cs_ready, wpT_ready, kv_used = (
            sem(n) for n in ("csB_ready", "gated_projection_ready", "keys_values_used"))
        var2_ready, rstd2_ready, h2_ready, h2_stored = (
            sem(n) for n in ("var2_ready", "rstd2_ready", "h2_ready", "h2_stored"))
        sel_ready, recs_ready, lists_clear, listed = (
            sem(n) for n in ("chosen_ready", "records_ready", "lists_clear", "listed"))
        base_ready, zero_ready, sums_clear = sem("base_ready"), sem("zeros_ready"), sem("token_sums_clear")
        mapf_ready = sem("map_columns_ready")
        tok_loaded = [sem(f"block_tokens_loaded{s}") for s in range(R)]
        dest_loaded = [sem(f"block_dests_loaded{s}") for s in range(R)]
        gathered = [sem(f"gathered{s}") for s in range(R)]
        scattered = [sem(f"scattered{s}") for s in range(R)]
        x_turned, xT_copied, gu_done, silu_done, act_done, act_turned, aT_copied, y_done, y_scaled = (
            sem(n) for n in ("x_turned", "xT_copied", "gate_up_done", "silu_done", "act_done", "act_turned", "aT_copied", "y_done", "y_scaled"))
        OT = 2
        POOL_ADDS = (1, 3, 5, 6)
        fetched = [sem(f"sums_fetched{g}") for g in range(NT // OT)]
        pool_added, out_ready, stored = sem("gpsimd_sums_added"), sem("out_ready"), sem("out_stored")

        use = {}
        uses = [0] * 8

        def plan(key, bank):
            uses[bank] += 1
            use[key] = bank, uses[bank]

        def plan_modulation(b):
            for s in range(2):
                plan(("mod", b, s), 2 + s)

        def plan_projection():
            for k in range(KC):
                plan(("wpT", k), k)

        def plan_tokens(b, g):
            for k in range(KC):
                plan(("hT", b, g, k), k)

        def plan_queries(b, g, bank):
            for k in range(KC):
                plan(("q", b, g, k), bank + k)

        def plan_tile(b, i):
            plan(("kv", b, i), 4 + i % 2)

        def plan_tiles(b, g):
            for i in range(g * GT, (g + 1) * GT):
                plan_tile(b, i)

        def plan_v_k(b):
            for k in range(KC):
                plan(("vk", b, k), 6 + k)

        def plan_attend(b):
            for i in range(TB):
                plan(("o", b, i), 2 + i % 2)
                plan(("oT", b, i), i % 2)
                plan(("proj", b, i), 4 + i % 2)
            if b == 0:
                for k in range(KC):
                    plan(("hT", 1, 0, k), 6 + k)
                for k in range(KC):
                    plan(("q", 1, 0, k), 6 + k)

        def plan_turn(b, g):
            for k in range(KC):
                plan(("h2T", b, g, k), k)
            if g == 0:
                plan(("router", b), 2)

        def plan_ranks(b):
            plan(("ranks", b), 3)

        def plan_hidden(b, g, pairs):
            for m in range(len(SC)):
                plan(("sg", b, g, m), pairs[m])
                plan(("su", b, g, m), pairs[m] + 1)

        def plan_rows(b, g, banks_of):
            for i in range(GT):
                plan(("sd", b, g * GT + i), banks_of[i % len(banks_of)])

        plan(("c",), 7)
        for g in range(2 * KC):
            plan(("wT", g), 3 + g % 2)
        plan(("modT",), 2)
        plan_tokens(0, 0)
        plan_queries(0, 0, 2)
        plan_tiles(0, 0)
        plan_tokens(0, 1)
        plan_modulation(0)
        plan_queries(0, 1, 0)
        for i in range(GT, TB):
            plan_tile(0, i)
            if i == TB - 3:
                plan_modulation(1)
            if i == TB - 2:
                plan_projection()
        plan_v_k(0)
        plan_attend(0)
        plan_turn(0, 0)
        for i in range(GT):
            if i == GT // 2:
                plan_turn(0, 1)
            plan_tile(1, i)
        plan_tokens(1, 1)
        plan_queries(1, 1, 2)
        plan_ranks(0)
        plan_tiles(1, 1)
        plan_v_k(1)
        plan_attend(1)
        for g in range(NG):
            plan_turn(1, g)
        plan_hidden(0, 0, (4, 6, 0))
        plan_ranks(1)
        plan_rows(0, 0, (4, 5, 6, 7))
        plan_hidden(0, 1, (0, 2, 6))
        plan_rows(0, 1, (4, 5))
        plan(("map",), 6)
        for g in range(NG):
            plan_hidden(1, g, (0, 2, 0))
            plan_rows(1, g, (4, 5))

        def of(key):
            return banks[use[key][0]]

        def fill(pe, key):
            bank, n = use[key]
            if n > 1:
                pe.wait_ge(drained[bank], n - 1)
            return banks[bank]

        def await_result(eng, key):
            bank, n = use[key]
            eng.wait_ge(filled[bank], n)
            return banks[bank]

        def full(key):
            return filled[use[key][0]]

        def free(key):
            return drained[use[key][0]]

        def await_computed(eng, key):
            eng.wait_ge(full(key), use[key][1])

        def await_read(eng, key):
            eng.wait_ge(free(key), use[key][1])

        def wait(eng, s, value):
            if not isinstance(value, int) or value > 0:
                eng.wait_ge(s, value)

        def first(n):
            return isinstance(n, int) and n == 0

        def load_last_turn(eng):
            return 1 + eng.value_load(map_i[0:1, 2 * MAP_W:2 * MAP_W + 1], min_val=FEWEST - 1, max_val=TURNS - 2)

        def load_values(eng, which, section, turn, first):
            _, values = nc.values_load_multi_w_load_instructions(
                map_i[0:1, bass.ds(section * MAP_W + 1 + first + R * turn, 2 * R)], engines=(which,),
                min_val=0, max_val=(E - 1, EMPTY)[section],
                skip_runtime_bounds_check_because="the map's entries are clamped where they are made")
            return values

        def blocks(eng, step):
            last_turn = load_last_turn(eng)
            step(0, False)
            with eng.Fori(1, FEWEST) as turn:
                step(turn, False)
            with eng.Fori(0, (TURNS - FEWEST) // 2) as two:
                turn = two * 2 + FEWEST
                with eng.If(turn < last_turn):
                    step(turn, False)
                    with eng.If(turn + 1 < last_turn):
                        step(turn + 1, False)
            step(last_turn, True)
            return last_turn

        block = ctx.enter_context(nc.Block())

        @block.sync
        def _(sp):
            sp.dma_start(c_row, cond).then_inc(ld_c, 16)
            sp.dma_start(wqkv_raw, w_qkv.rearrange("(o p) c -> p o c", p=P)).then_inc(ld_qkv, 16)
            w_mod_v = w_mod.rearrange("(k p) n -> p k n", p=P)
            sp.dma_start(wmod_sb[:, :, 0:2 * C], w_mod_v[:, :, 0:2 * C]).then_inc(ld_mod, 16)
            sp.dma_start(X[:, 0:GT, :], x_v[:, 0, 0:GT, :]).then_inc(ld_x[0], 16)
            sp.dma_start(X[:, GT:2 * GT, :], x_v[:, 0, GT:2 * GT, :]).then_inc(ld_x[1], 16)
            sp.dma_start(wmod_sb[:, :, 2 * C:], w_mod_v[:, :, 2 * C:]).then_inc(ld_mod_rows, 16)
            sp.dma_start(wproj_raw, w_proj.rearrange("(o p) c -> p o c", p=P)).then_inc(ld_proj, 16)
            sp.dma_start(bga[:, 0, :], b_proj.partition_broadcast(P)).then_inc(ld_proj, 16)
            for g in range(2, NT // GT):
                sp.dma_start(X[:, g * GT:(g + 1) * GT, :], x_v[:, g // NG, g % NG * GT:(g % NG + 1) * GT, :]).then_inc(ld_x[g], 16)
            sp.dma_start(router[:, :, :], w_router.rearrange("(k p) e -> p k e", p=P)).then_inc(ld_route, 16)
            sp.dma_start(bias_bc[:, :], corr_bias.partition_broadcast(P)).then_inc(ld_route, 16)
            for a, w in enumerate((sh_gate_w, sh_up_w)):
                sp.dma_start(sh_gu[:, a, :, :], w.rearrange("(k p) m -> p k m", p=P)).then_inc(ld_sh, 16)
            for m, (a, n) in enumerate(SC):
                sp.dma_start(sh_dn[0:n, m, :], sh_down_w[a:a + n, :]).then_inc(ld_sh, 16)
            sp.wait_ge(zero_ready, 1)
            for a in range(2):
                sp.dma_start(token_sums[a].rearrange("(p n) c -> p n c", p=P),
                             h2[:, 0:1, :].broadcast_to([P, NT, C])).then_inc(sums_clear, 16)
            sp.wait_ge(consts, 5)
            sp.dma_start(lists.rearrange("(p n) w -> p (n w)", p=P), empties).then_inc(lists_clear, 16)

            def load_gate_up(e0, e1, s):
                for a, w in enumerate((gate_w, up_w)):
                    for k in range(KC):
                        sp.dma_start(gu_v[:, e0:e1, k, a * M:(a + 1) * M],
                                     w[e0:e1, k * P:(k + 1) * P, :].rearrange("e p m -> p e m")).then_inc(s, 16)

            for e in range(0, EARLY, 8):
                load_gate_up(e, e + 8, ld_early)
            for b in range(B):
                for g in range(NG):
                    sp.wait_ge(h2_ready, b * TB + (g + 1) * GT)
                    sp.dma_start(h2_tiles[:, b, g * GT:(g + 1) * GT, :], h2[:, g * GT:(g + 1) * GT, :]).then_inc(h2_stored, 16)
            sp.wait_ge(h2_stored, 16 * B * NG)
            await_computed(sp, ("h2T", B - 1, NG - 1, KC - 1))
            sp.wait_ge(recs_ready, 2 * B)
            sp.wait_ge(mapf_ready, 1)
            for m in range(2):
                sp.dma_start(dn_v[0:KD, m, :].rearrange("p (e c) -> p e c", e=E),
                             down_w[:, m * KD:(m + 1) * KD, :].rearrange("e p c -> p e c")).then_inc(ld_late, 16)
            load_gate_up(EARLY, E, ld_late)
            sp.wait_ge(listed, 16 * NT * TOPK)
            await_read(sp, ("map",))

            def load_records(ring, c, col, loaded):
                sp.dma_start(ring[:, c, :], lists[bass.ds(col * P, P), :]).then_inc(loaded[c], 16)

            SP = mybir.EngineType.SP
            cols = load_values(sp, SP, 1, 0, 0)
            for c in range(R):
                load_records(tok_rec, c, cols[c], tok_loaded)

            def step(turn, last):
                cols = load_values(sp, SP, 1, turn, 0)
                for c in range(R):
                    wait(sp, scattered[c], 16 * turn)
                    load_records(dest_rec, c, cols[c], dest_loaded)
                    if not last:
                        sp.wait_ge(gathered[c], 16 * turn + 16)
                        load_records(tok_rec, c, cols[c + R], tok_loaded)

            last_turn = blocks(sp, step)
            def fetch_sums(a, g):
                t = g * OT
                sp.dma_start(sums[:, a, t:t + OT, :], sums_v[a][:, t // TB, t % TB:t % TB + OT, :]).then_inc(fetched[g], 16)

            early = 2
            for a in range(2):
                for s in range(a, R, 2):
                    sp.wait_ge(scattered[s], 16 * last_turn + 16)
                for g in range(early):
                    fetch_sums(a, g)
            for g in range(early, NT // OT):
                for a in range(2):
                    fetch_sums(a, g)
            for g in range(NT // OT):
                t = g * OT
                sp.wait_ge(out_ready, g + 1)
                sp.dma_start(out_v[:, t // TB, t % TB:t % TB + OT, :], X[:, t:t + OT, :]).then_inc(stored, 16)
            sp.wait_ge(stored, 16 * NT // OT)

        @block.gpsimd
        def _(pool):
            done = [0]

            def link(ins):
                done[0] += 1
                ins.then_inc(pool_own, 1)
                pool.wait_ge(pool_own, done[0])

            nc.gpsimd.memset(h2[:, 0, :], 0.0).then_inc(zero_ready, 1)
            link(nc.gpsimd.memset(ident[:, :], 0.0))
            nc.gpsimd.affine_select(out=ident[:, :], in_=ident[:, :], compare_op=ALU.not_equal, fill=1.0,
                                    base=0, pattern=[[-1, P]], channel_multiplier=1).then_inc(ident_ready, 1)
            link(nc.gpsimd.memset(minus_half[:, :], -0.5))

            def power(out_ap, var_ap, n):
                link(nc.gpsimd.tensor_scalar(out_ap, var_ap, LN_EPS, None, ALU.add))
                return nc.gpsimd.tensor_tensor(out_ap, out_ap, minus_half[:, 0:n], ALU.pow)

            def first_deviation(g):
                a, z = g * GT, (g + 1) * GT
                pool.wait_ge(var_ready, z)
                power(rstd[:, a:z], mv[:, a:z, 1], GT).then_inc(rstd_ready, 1)

            first_deviation(0)
            link(nc.gpsimd.memset(ones_bf[:, :], 1.0))
            nc.gpsimd.affine_select(out=tri[:, :], in_=ones_bf[:, :], compare_op=ALU.is_gt, fill=0.0,
                                    base=0, pattern=[[1, P]], channel_multiplier=-1).then_inc(consts, 1)
            nc.gpsimd.iota(iota_e[:, :], [[1, E]], base=0, channel_multiplier=0,
                           allow_small_or_imprecise_dtypes=True).then_inc(consts, 1)
            nc.gpsimd.iota(iota_p[:, :], [[1, 1]], base=0, channel_multiplier=1,
                           allow_small_or_imprecise_dtypes=True).then_inc(consts, 1)
            nc.gpsimd.memset(vv[:, :, :, HD:VE], 1.0).then_inc(consts, 1)
            link(nc.gpsimd.memset(empties, 0.0))
            empty_dests = empties.rearrange("p (n w) -> p n w", w=4)[:, :, 1:2].bitcast(i32)
            nc.gpsimd.iota(empty_dests, [[0, NCOL]], base=T, channel_multiplier=1).then_inc(consts, 1)
            link(nc.gpsimd.memset(recs[:, :, :, :], 0.0))
            for b in range(B):
                for a in range(2):
                    last = nc.gpsimd.iota(recs[:, b * TB:(b + 1) * TB, :, a:a + 1].bitcast(i32), [[1, TB], [0, TOPK]],
                                          base=b * N, channel_multiplier=TB)
            last.then_inc(consts, 1)
            nc.gpsimd.memset(used[:, :], 0.0)
            nc.gpsimd.iota(iota_n[:, :], [[P, NT]], base=0, channel_multiplier=0,
                           allow_small_or_imprecise_dtypes=True).then_inc(consts, 1)
            nc.gpsimd.memset(nd, 0.0).then_inc(consts, 1)
            link(nc.gpsimd.memset(later[:, :, :], 1.0))
            nc.gpsimd.memset(later[:, :, 0:1], 0.0).then_inc(consts, 1)

            for g in range(1, NT // GT):
                first_deviation(g)
            pool.wait_ge(wpT_ready, 1)
            for t in range(NT):
                pool.wait_ge(xn_ready, t + 1)
                nc.gpsimd.tensor_tensor(X[:, t, :], X[:, t, :], bga[:, t // TB, :], ALU.add).then_inc(xb_ready, 1)

            def second_deviation(b, g):
                a = b * TB + g * GT
                pool.wait_ge(var2_ready, a + GT)
                power(rstd2[:, a:a + GT], mv2[:, a:a + GT, 1], GT).then_inc(rstd2_ready, 1)

            def list_pairs(a, z):
                if a == 0:
                    pool.wait_ge(lists_clear, 16)
                for n in range(a, z):
                    t, k = n // TOPK, n % TOPK
                    pool.wait_ge(recs_ready, t // GT + 1)
                    nc.gpsimd.indirect_dma_start(
                        out=lists, out_offset=bass.IndirectOffsetOnAxis(ap=rows_i[:, t, k:k + 1], axis=0),
                        in_=recs[:, t, k, :], in_offset=None).then_inc(listed, 16)

            second_deviation(0, 0)
            second_deviation(0, 1)
            list_pairs(0, 15)
            second_deviation(1, 0)
            list_pairs(15, 22)
            second_deviation(1, 1)
            list_pairs(22, NT * TOPK)

            pool.wait_ge(h2_stored, 16 * B * NG)
            await_computed(pool, ("sd", 0, TB - 1))

            await_read(pool, ("map",))

            def fetch(s):
                nc.gpsimd.indirect_dma_start(
                    out=xg[:, s, :], out_offset=None, in_=h2_dram,
                    in_offset=bass.IndirectOffsetOnAxis(ap=tok_rec[:, s, 0:1].bitcast(i32), axis=0)).then_inc(gathered[s], 16)

            for s in range(R):
                pool.wait_ge(tok_loaded[s], 16)
                fetch(s)

            def gather_next(c, turn):
                pool.wait_ge(tok_loaded[c], 16 * turn + 32)
                pool.wait_ge(x_turned, R * turn + c + 1)
                pool.sem_inc(pool_passed, 1)
                fetch(c)

            def scatter(c, n, turns):
                pool.wait_ge(y_scaled, n + 1)
                wait(pool, scattered[(c - 2) % R], 16 * turns)
                pool.sem_inc(pool_passed, 1)
                nc.gpsimd.indirect_dma_start(
                    out=token_sums[c % 2], out_offset=bass.IndirectOffsetOnAxis(ap=dest_rec[:, c, 1:2].bitcast(i32), axis=0),
                    in_=yw[:, c, :], in_offset=None, bounds_check=T - 1, oob_is_err=False,
                    compute_op=ALU.add).then_inc(scattered[c], 16)

            def step(turn, last):
                for c in range(R):
                    n = R * turn + c
                    if not last:
                        gather_next(c, turn)
                    if not first(n):
                        scatter((c - 1) % R, n - 1, turn + (c == R - 1))
                    if last and c == R - 1:
                        scatter(c, n, turn + 1)

            blocks(pool, step)

            for g in POOL_ADDS:
                pool.wait_ge(fetched[g], 32)
                total = sums[:, 0, g * OT:(g + 1) * OT, :]
                nc.gpsimd.tensor_tensor(total, total, sums[:, 1, g * OT:(g + 1) * OT, :], ALU.add).then_inc(pool_added, 1)

        @block.scalar
        def _(act_e):
            ps = await_result(act_e, ("c",))
            nc.scalar.activation(csT, ps[:, 0:KC * B].rearrange("p (k b) -> p k b", k=KC),
                                 ACT.Silu).then_inc(free(("c",)), 1)

            for g in range(2 * KC):
                key = ("wT", g)
                ps = await_result(act_e, key)
                n = 3 * C // 2
                nc.scalar.activation(wT[:, g // 2, (g % 2) * n:(g % 2 + 1) * n], ps[:, 0:n], ACT.Copy).then_inc(free(key), 1)

            def tokens(b, g):
                for k in range(KC):
                    key = ("hT", b, g, k)
                    ps = await_result(act_e, key)
                    if b == 0 and g == 0 and k == 0:
                        await_read(act_e, ("modT",))
                    nc.scalar.activation(hT[:, k, :], ps[:, :], ACT.Identity, bias=modT[:, k, b:b + 1],
                                         scale=modT[:, KC + k, b:b + 1]).then_inc(free(key), 1)

            def queries(b, g, k):
                key = ("q", b, g, k)
                ps = await_result(act_e, key)
                if b >= 1:
                    await_computed(act_e, ("o", b - 1, (g + 1) * GT - 1))
                nc.scalar.activation(qT[:, k, g * W:(g + 1) * W], ps[:, :], ACT.Relu).then_inc(free(key), 1)

            def head(b, g):
                tokens(b, g)
                for k in range(KC):
                    queries(b, g, k)

            def tile(b, i):
                t = b * TB + i
                key = ("kv", b, i)
                ps = await_result(act_e, key)
                if t >= 2:
                    if (t - 2) % TB == TB - 1:
                        await_computed(act_e, ("vk", (t - 2) // TB, KC - 1))
                    else:
                        act_e.wait_ge(kv_used, t - 1 - (t - 2) // TB)
                if t == 0:
                    act_e.wait_ge(consts, 8)
                nc.scalar.activation(kk[:, t % 2, :], ps[:, 0:C], ACT.Relu)
                nc.scalar.activation(vv[:, t % 2, :, 0:HD], ps[:, C:2 * C].rearrange("p (h e) -> p h e", h=NH),
                                     ACT.Copy).then_inc(free(key), 1)

            def tiles(b, g):
                for i in range(g * GT, (g + 1) * GT):
                    tile(b, i)

            def attend(b):
                for i in range(TB):
                    key = ("oT", b, i)
                    ps = await_result(act_e, key)
                    if i >= 2:
                        await_computed(act_e, ("proj", b, i - 2))
                    nc.scalar.activation(oT[:, i % 2], ps[:, 0:C].rearrange("p (k n) -> p k n", k=KC),
                                         ACT.Copy).then_inc(free(key), 1)
                    if b == 0:
                        beside(i + 1)

            def beside(i):
                if i == 2:
                    tokens(1, 0)
                if i == 4:
                    queries(1, 0, 0)
                if i == 6:
                    queries(1, 0, 1)

            def load_sigmoid():
                nc.scalar.activation(sigmoid_table[:, :], iota_p[:, :], ACT.Sigmoid)

            def turned(b, g):
                for k in range(KC):
                    key = ("h2T", b, g, k)
                    ps = await_result(act_e, key)
                    nc.scalar.activation(h2T[:, b, k, g * W:(g + 1) * W], ps[:, :], ACT.Copy).then_inc(free(key), 1)

            def scores(b):
                key = ("router", b)
                ps = await_result(act_e, key)
                if b == 0:
                    act_e.wait_ge(lists_clear, 16)
                else:
                    act_e.wait_ge(recs_ready, 2)
                nc.scalar.activation(score, ps[:, 0:TB * E].rearrange("p (i e) -> p i e", i=TB),
                                     ACT.Sigmoid).then_inc(free(key), 1)

            def hidden(b):
                for g in range(NG):
                    for m, (a, n) in enumerate(SC):
                        key = ("sg", b, g, m)
                        ps = await_result(act_e, key)
                        if (b, g) != (0, 0) and m == 0:
                            await_computed(act_e, ("sd", b, g * GT - 1) if g else ("sd", b - 1, TB - 1))
                        nc.scalar.activation(sT[0:n, m, :], ps[0:n, :], ACT.Silu).then_inc(free(key), 1)

            head(0, 0)
            tiles(0, 0)
            head(0, 1)
            tiles(0, 1)
            attend(0)
            load_sigmoid()
            turned(0, 0)
            for i in range(GT // 2):
                tile(1, i)
            turned(0, 1)
            scores(0)
            for i in range(GT // 2, GT):
                tile(1, i)
            head(1, 1)
            tiles(1, 1)
            attend(1)
            load_sigmoid()
            for g in range(NG):
                turned(1, g)
            scores(1)
            hidden(0)
            hidden(1)

            def silu(c, n):
                act_e.wait_ge(gu_done, n + 1)
                if not isinstance(n, int) or n >= 2:
                    act_e.wait_ge(act_done, n - 1)
                nc.scalar.activation(act_g[:, c % 2, :], banks[1 + c % 2][:, 0:M], ACT.Silu).then_inc(silu_done, 1)

            def copy_act(c, n):
                act_e.wait_ge(act_turned, n + 1)
                wait(act_e, y_done, n - 1)
                nc.scalar.activation(aT[0:KD, c % 2, :, :], banks[3][0:KD, 0:2 * P].rearrange("p (m n) -> p m n", m=2),
                                     ACT.Copy).then_inc(aT_copied, 1)

            def weigh(c, n, turns):
                act_e.wait_ge(y_done, n + 1)
                act_e.wait_ge(dest_loaded[c], 16 * turns)
                nc.scalar.activation(yw[:, c, :], banks[4 + c % 2][:, 0:C], ACT.Copy,
                                     scale=dest_rec[:, c, 2:3]).then_inc(y_scaled, 1)

            await_read(act_e, ("map",))
            silu(0, 0)

            def step(turn, last):
                for c in range(R):
                    n = R * turn + c
                    if not last or c + 1 < R:
                        silu(c + 1, n + 1)
                    copy_act(c, n)
                    if not first(n):
                        weigh((c - 1) % R, n - 1, turn + (c > 0))
                    if last and c == R - 1:
                        weigh(c, n, turn + 1)

            blocks(act_e, step)

        @block.vector
        def _(dve):
            done = [0]

            def link(ins):
                done[0] += 1
                ins.then_inc(dve_own, 1)
                dve.wait_ge(dve_own, done[0])

            def mark(ins):
                done[0] += 1
                ins.then_inc(dve_own, 1)
                return done[0]

            def after(count):
                dve.wait_ge(dve_own, count)

            def link_free(ins, key):
                ins.then_inc(free(key), 1)
                await_read(dve, key)

            V = nc.vector

            def first_norm(g):
                dve.wait_ge(ld_x[g], 16)
                for t in range(g * GT, (g + 1) * GT):
                    link(V.bn_stats(stats[:, t, :], X[:, t, :]))
                    V.bn_aggr(mv[:, t, :], stats[:, t, :]).then_inc(var_ready, 1)

            def normalise(g):
                dve.wait_ge(rstd_ready, g + 1)
                dve.wait_ge(var_ready, (g + 1) * GT)
                for t in range(g * GT, (g + 1) * GT):
                    V.tensor_scalar(xn[:, t, :], X[:, t, :], mv[:, t, 0:1], rstd[:, t:t + 1],
                                    ALU.subtract, ALU.mult).then_inc(xn_ready, 1)

            first_norm(0)
            normalise(0)
            await_read(dve, ("c",))
            V.tensor_copy(csB, csT.unsqueeze(3).broadcast_to([P, KC, B, P])).then_inc(cs_ready, 1)
            ps = await_result(dve, ("modT",))
            link(V.tensor_copy(modT[:, 0:KC, :], ps[:, 0:KC * B].rearrange("p (k b) -> p k b", k=KC)))
            V.tensor_scalar(modT[:, KC:2 * KC, :], ps[:, KC * B:2 * KC * B].rearrange("p (k b) -> p k b", k=KC),
                            1.0, None, ALU.add).then_inc(free(("modT",)), 1)
            for g in range(1, NT // GT):
                first_norm(g)
            for g in range(1, NT // GT):
                normalise(g)
            for b in range(B):
                for s in range(2):
                    key = ("mod", b, s)
                    ps = await_result(dve, key)
                    gate = rows[:, b, 0, :] if s == 0 else gb[:, b, :]
                    src = ps[:, 0:C] if s == 0 else ps[:, C:2 * C]
                    other = ps[:, C:2 * C] if s == 0 else ps[:, 0:C]
                    link(V.tensor_scalar(rows[:, b, 3, :], src, -1.0, GUARD, ALU.mult, ALU.max))
                    link(V.tensor_tensor(rows[:, b, 3, :], src, rows[:, b, 3, :], ALU.max))
                    link(V.tensor_scalar(gate, src, 0.0, 2.0, ALU.is_ge, ALU.mult))
                    V.tensor_scalar(rows[:, b, 1 + s, :], other, float(s), None, ALU.add).then_inc(free(key), 1)
                    link(V.scalar_tensor_tensor(out=gate, in0=gate, scalar=-1.0, in1=rows[:, b, 3, :],
                                                op0=ALU.add, op1=ALU.mult))
            for k in range(KC):
                key = ("wpT", k)
                ps = await_result(dve, key)
                for b in range(B):
                    last = V.tensor_tensor(wpT[:, b, k, :], ps[:, 0:C], rows[:, b, 0, :], ALU.mult)
                last.then_inc(free(key), 1)
            dve.wait_ge(ld_proj, 32)
            link(V.tensor_tensor(bga[:, 1, :], bga[:, 0, :], rows[:, 1, 0, :], ALU.mult))
            V.tensor_tensor(bga[:, 0, :], bga[:, 0, :], rows[:, 0, 0, :], ALU.mult).then_inc(wpT_ready, 1)

            def attend(b):
                for k in range(KC):
                    key = ("vk", b, k)
                    ps = await_result(dve, key)
                    if b == 0:
                        dve.wait_ge(consts, 8)
                    for h in range(HH):
                        r, c = slice(h * HD, (h + 1) * HD), slice(h * VE, (h + 1) * VE)
                        last = V.tensor_copy(nd[r, k, c], ps[r, c])
                    last.then_inc(free(key), 1)
                for i in range(TB + 3):
                    tile_step(b, i)
                    if i == 2 * GT:
                        second_norm(b, 0)
                second_norm(b, 1)

            def tile_step(b, i):
                heads_here, rows_here = i < TB, i >= 3
                if heads_here:
                    heads_key = ("o", b, i)
                    heads = await_result(dve, heads_key)[:, 0:NH * VE].rearrange("p (h e) -> p h e", h=NH)
                    weight_sum = mark(V.tensor_scalar(rden[:, i % 2, :], heads[:, :, HD], DIV_EPS, None, ALU.add))
                if rows_here:
                    t = b * TB + i - 3
                    rows_key = ("proj", b, i - 3)
                    ps = await_result(dve, rows_key)
                    dve.wait_ge(xb_ready, t + 1)
                    V.tensor_tensor(X[:, t, :], ps[:, 0:C], X[:, t, :], ALU.add).then_inc(free(rows_key), 1)
                if heads_here:
                    after(weight_sum)
                    inverse = mark(V.reciprocal(rden[:, i % 2, :], rden[:, i % 2, :]))
                if rows_here:
                    await_read(dve, rows_key)
                    statistics = mark(V.bn_stats(stats[:, t, :], X[:, t, :]))
                if heads_here:
                    after(inverse)
                    if i >= 2:
                        await_computed(dve, ("oT", b, i - 2))
                    V.tensor_tensor(o[:, i % 2, :].rearrange("p (h e) -> p h e", h=NH), heads[:, :, 0:HD],
                                    rden[:, i % 2, :].unsqueeze(2).broadcast_to([P, NH, HD]), ALU.mult).then_inc(free(heads_key), 1)
                if rows_here:
                    after(statistics)
                    V.bn_aggr(mv2[:, t, :], stats[:, t, :]).then_inc(var2_ready, 1)

            def second_norm(b, g):
                if b == 0 and g == 0:
                    dve.wait_ge(sums_clear, 32)
                dve.wait_ge(rstd2_ready, b * NG + g + 1)
                dve.wait_ge(var2_ready, b * TB + (g + 1) * GT)
                if b == 1 and g == 0:
                    dve.wait_ge(h2_stored, 16 * NG)
                    await_computed(dve, ("h2T", 0, NG - 1, KC - 1))
                for i in range(g * GT, (g + 1) * GT):
                    t = b * TB + i
                    last = V.scalar_tensor_tensor(out=h2[:, i, :], in0=X[:, t, :], scalar=mv2[:, t, 0:1],
                                                  in1=rows[:, b, 2, :], op0=ALU.subtract, op1=ALU.mult)
                link(last)
                for i in range(g * GT, (g + 1) * GT):
                    t = b * TB + i
                    V.scalar_tensor_tensor(out=h2[:, i, :], in0=h2[:, i, :], scalar=rstd2[:, t:t + 1],
                                           in1=rows[:, b, 1, :], op0=ALU.mult, op1=ALU.add).then_inc(h2_ready, 1)

            def over(ap, shape, axis):
                return ap.unsqueeze(axis).broadcast_to(shape)

            def choose(b):
                shape = [P, TB, E]
                key = ("router", b)
                await_read(dve, key)
                if b == 0:
                    dve.wait_ge(ld_route, 32)
                link(V.tensor_tensor(sfc, score, over(bias_bc[:, :], shape, 1), ALU.add))
                q = sfc.rearrange("p i (g j) -> p (i g) j", j=EG)
                pairs = sfc.rearrange("p i (g h l) -> p (i g) h l", h=2, l=2)
                larger, both = pair[:, 0], pair[:, 1]
                V.tensor_tensor(larger, pairs[:, :, :, 0], pairs[:, :, :, 1], ALU.max)
                link(V.tensor_tensor(both, pairs[:, :, :, 0], pairs[:, :, :, 1], ALU.add))
                g_flat = gs.rearrange("p i g -> p (i g)")
                link(V.tensor_tensor(g_flat, larger[:, :, 0], larger[:, :, 1], ALU.add))
                link(V.tensor_tensor(g_flat, g_flat, both[:, :, 0], ALU.max))
                link(V.tensor_tensor(g_flat, g_flat, both[:, :, 1], ALU.max))

                def largest(values, n, width):
                    for i in range(TB):
                        last = V.max(top[:, i, :], values[:, i, :])
                    link(last)
                    for i in range(TB):
                        last = V.max_index(top_i[:, i, :], top[:, i, :], values[:, i, :])
                    link(last)
                    link(V.tensor_copy(top_f, top_i[:, :, :]))
                    one = chosen[:, :, 0:n, 0:width]
                    s4 = [P, TB, n, width]
                    return one, V.tensor_tensor(one, iota_e[:, 0:width].unsqueeze(1).unsqueeze(1).broadcast_to(s4),
                                                top_f[:, :, 0:n].unsqueeze(3).broadcast_to(s4), ALU.is_equal)

                if b == 0:
                    dve.wait_ge(consts, 9)
                else:
                    await_computed(dve, ("ranks", 0))
                one, compared = largest(gs, TOPG, G)
                link(compared)
                link(V.tensor_reduce(gmask, one.rearrange("p i k g -> p i g k"), AX.X, ALU.add))
                link(V.tensor_scalar(gmask, gmask, -0.5, -2 * LOW, ALU.add, ALU.mult))
                m_q = sel.rearrange("p i (g j) -> p (i g) j", j=EG)
                link(V.tensor_tensor(m_q, q, gmask.rearrange("p i g -> p (i g)").unsqueeze(2).broadcast_to([P, TB * G, EG]),
                                     ALU.min))
                one, compared = largest(sel, TOPK, E)
                compared.then_inc(sel_ready, 1)
                dve.wait_ge(sel_ready, b + 1)

            def summed(values, half, out_ap):
                s4 = [P, GT, TOPK, E]
                tiles = slice(half * GT, (half + 1) * GT)
                link(V.tensor_tensor(weighed[:, tiles], chosen[:, tiles], over(values[:, tiles, :], s4, 2), ALU.mult))
                link(V.tensor_reduce(out_ap, weighed[:, tiles], AX.X, ALU.add))

            def weights(b, half):
                t = b * TB + half * GT
                summed(score, half, recs[:, t:t + GT, :, 2])

            def place(b):
                key = ("ranks", b)
                ps = await_result(dve, key)
                w = TB * E
                in_tile = ps[:, 0:w].rearrange("p (i e) -> p i e", i=TB)
                V.tensor_tensor(rank, in_tile, over(used[:, :], [P, TB, E], 1), ALU.add)
                link_free(V.tensor_tensor_scan(before.rearrange("p e i -> p (e i)"), later[:, :, :].rearrange("p e i -> p (e i)"),
                                                 ps[:, w:2 * w], 0.0, ALU.mult, ALU.add), key)
                link(V.tensor_tensor(rank[:, 1:TB, :], rank[:, 1:TB, :],
                                     before[:, :, 0:TB - 1].rearrange("p e i -> p i e"), ALU.add))
                V.tensor_tensor(used[:, :], used[:, :], before[:, :, TB - 1], ALU.add)
                link(V.scalar_tensor_tensor(out=rank, in0=over(iota_e[:, :], [P, TB, E], 1), scalar=float(T), in1=rank,
                                            op0=ALU.mult, op1=ALU.add))

            def list_rows(b, half):
                t = b * TB + half * GT
                tiles = slice(half * GT, (half + 1) * GT)
                summed(rank, half, top_f[:, tiles, 0:TOPK])
                V.tensor_copy(rows_i[:, t:t + GT, :], top_f[:, tiles, 0:TOPK]).then_inc(recs_ready, 1)

            def records(b):
                weights(b, 0)
                place(b)
                list_rows(b, 0)
                if b == 1:
                    hidden(0, 0)
                weights(b, 1)
                list_rows(b, 1)

            def hidden(b, g):
                for m, (a, n) in enumerate(SC):
                    key = ("su", b, g, m)
                    ps = await_result(dve, key)
                    await_read(dve, ("sg", b, g, m))
                    V.tensor_tensor(sT[0:n, m, :], sT[0:n, m, :], ps[0:n, :], ALU.mult).then_inc(free(key), 1)

            def shared_rows(b, g):
                for i in range(g * GT, (g + 1) * GT):
                    t = b * TB + i
                    key = ("sd", b, i)
                    ps = await_result(dve, key)
                    link_free(V.tensor_tensor(sh_tmp[:, :], ps[:, 0:C], gb[:, b, :], ALU.mult), key)
                    V.tensor_tensor(X[:, t, :], X[:, t, :], sh_tmp[:, :], ALU.add).then_inc(base_ready, 1)
                    dve.wait_ge(base_ready, t + 1)

            attend(0)
            choose(0)
            records(0)
            attend(1)
            choose(1)
            records(1)
            shared_rows(0, 0)

            shape = [P, E, NT]
            link(V.tensor_tensor(more, used[:, :].unsqueeze(2).broadcast_to(shape),
                                 iota_n[:, :].unsqueeze(1).broadcast_to(shape), ALU.is_gt))
            link(V.tensor_reduce(seg[:, 0, :], more, AX.X, ALU.add))
            link(V.memset(seg[:, 2, :], 1.0))
            link(V.tensor_tensor_scan(seg[:, 1, :], seg[:, 2, :], seg[:, 0, :], 0.0, ALU.mult, ALU.add))
            link(V.tensor_tensor(seg[:, 0, :], seg[:, 1, :], seg[:, 0, :], ALU.subtract))
            link(V.tensor_scalar(seg[:, 2, :], seg[:, 1, :], iota_p[:, 0:1], None, ALU.is_le))
            link(V.tensor_reduce(mapf[:, 0:1], seg[:, 2, :], AX.X, ALU.add))
            link(V.tensor_scalar(mapf[:, 0:1], mapf[:, 0:1], float(E - 1), None, ALU.min))
            link(V.tensor_scalar(seg[:, 3, :], iota_e[:, :], mapf[:, 0:1], None, ALU.is_equal))
            link(V.scalar_tensor_tensor(out=seg[:, 0, :], in0=iota_e[:, :], scalar=float(NT), in1=seg[:, 0, :],
                                        op0=ALU.mult, op1=ALU.subtract))
            link(V.tensor_tensor(seg[:, 3, :], seg[:, 3, :], seg[:, 0, :], ALU.mult))
            link(V.tensor_reduce(mapf[:, 1:2], seg[:, 3, :], AX.X, ALU.add))
            link(V.tensor_tensor(mapf[:, 1:2], mapf[:, 1:2], iota_p[:, 0:1], ALU.add))
            link(V.tensor_tensor(mapf[:, 2:3], iota_p[:, 0:1], seg[:, 1, E - 1:E], ALU.is_ge))
            link(V.scalar_tensor_tensor(out=mapf[:, 1:2], in0=mapf[:, 2:3], scalar=2.0 * P * NT, in1=mapf[:, 1:2],
                                        op0=ALU.mult, op1=ALU.add))
            link(V.tensor_scalar(mapf[:, 1:2], mapf[:, 1:2], float(EMPTY), None, ALU.min))
            link(V.tensor_scalar(seg[:, 3, 0:TURNS], iota_e[:, 0:TURNS], float(R), None, ALU.mult))
            link(V.tensor_scalar(seg[:, 3, 0:TURNS], seg[:, 3, 0:TURNS], seg[:, 1, E - 1:E], None, ALU.is_lt))
            link(V.tensor_reduce(mapf[:, 2:3], seg[:, 3, 0:TURNS], AX.X, ALU.add))
            V.tensor_scalar(mapf[:, 2:3], mapf[:, 2:3], -2.0, None, ALU.add).then_inc(mapf_ready, 1)
            dve.wait_ge(mapf_ready, 1)
            hidden(0, 1)
            shared_rows(0, 1)
            await_computed(dve, ("map",))
            link(V.memset(map_i, 0))
            link(V.tensor_copy(map_i[0:1, 2 * MAP_W:2 * MAP_W + 1], mapf[0:1, 2:3]))
            ps = await_result(dve, ("map",))
            V.tensor_copy(map_i[0:1, 0:2 * MAP_W].rearrange("p (a n) -> p a n", a=2)[:, :, 1:P + 1],
                          ps[0:1, 0:2 * P].rearrange("p (a n) -> p a n", a=2)).then_inc(free(("map",)), 1)
            await_read(dve, ("map",))
            for g in range(NG):
                hidden(1, g)
                shared_rows(1, g)

            def copy_x(c, n):
                dve.wait_ge(x_turned, n + 1)
                if not isinstance(n, int) or n >= 2:
                    dve.wait_ge(gu_done, n - 1)
                V.tensor_copy(xT[:, c % 2], banks[0][:, 0:C].rearrange("p (k n) -> p k n", k=KC)).then_inc(xT_copied, 1)

            def multiply(c, n):
                dve.wait_ge(silu_done, n + 1)
                if not isinstance(n, int) or n >= 2:
                    dve.wait_ge(act_turned, n - 1)
                V.tensor_tensor(act[:, c % 2, :], act_g[:, c % 2, :], banks[1 + c % 2][:, M:M2], ALU.mult).then_inc(act_done, 1)

            for c in range(2):
                copy_x(c, c)
            multiply(0, 0)

            def step(turn, last):
                for c in range(R):
                    n = R * turn + c
                    if not last or c + 2 < R:
                        copy_x(c, n + 2)
                    if not last or c + 1 < R:
                        multiply(c + 1, n + 1)

            blocks(dve, step)

            for g in range(NT // OT):
                rows_g = slice(g * OT, (g + 1) * OT)
                total = sums[:, 0, rows_g, :]
                if g in POOL_ADDS:
                    dve.wait_ge(pool_added, POOL_ADDS.index(g) + 1)
                else:
                    dve.wait_ge(fetched[g], 32)
                    link(V.tensor_tensor(total, total, sums[:, 1, rows_g, :], ALU.add))
                link(V.tensor_tensor(total, total, over(gb[:, g * OT // TB, :], [P, OT, C], 1), ALU.mult))
                V.tensor_tensor(X[:, rows_g, :], X[:, rows_g, :], total, ALU.add).then_inc(out_ready, 1)

        @block.tensor
        def _(pe):
            mm = nc.tensor.matmul

            def turn(out_ap, in_ap):
                return nc.tensor.transpose(out_ap, in_ap, ident[:, :])

            pe.wait_ge(ident_ready, 1)
            pe.wait_ge(ld_c, 16)
            ps = fill(pe, ("c",))
            for k in range(KC):
                last = nc.tensor.transpose(ps[:, k * B:(k + 1) * B], c_row[:, k * P:(k + 1) * P], ident[0:B, 0:B])
            last.then_inc(full(("c",)), 1)
            pe.wait_ge(ld_qkv, 16)
            for g in range(2 * KC):
                ps = fill(pe, ("wT", g))
                for o3 in range(3):
                    last = turn(ps[:, o3 * P:(o3 + 1) * P], wqkv_raw[:, (g % 2) * 3 + o3, (g // 2) * P:(g // 2 + 1) * P])
                last.then_inc(full(("wT", g)), 1)
            pe.wait_ge(ld_mod, 16)
            await_read(pe, ("c",))
            ps = fill(pe, ("modT",))
            for j in range(2 * KC):
                for k in range(KC):
                    last = mm(ps[:, j * B:(j + 1) * B], wmod_sb[:, k, j * P:(j + 1) * P], csT[:, k, :],
                              start=k == 0, stop=k == KC - 1)
            last.then_inc(full(("modT",)), 1)

            def modulation(b):
                if b == 0:
                    pe.wait_ge(cs_ready, 1)
                    pe.wait_ge(ld_mod_rows, 16)
                for s in range(2):
                    ps = fill(pe, ("mod", b, s))
                    for k in range(KC):
                        a = 2 * C + s * 2 * C
                        last = mm(ps[:, :], csB[:, k, b, :], wmod_sb[:, k, a:a + 2 * C], start=k == 0, stop=k == KC - 1)
                    last.then_inc(full(("mod", b, s)), 1)

            def projection():
                pe.wait_ge(ld_proj, 32)
                for k in range(KC):
                    ps = fill(pe, ("wpT", k))
                    for j in range(KC):
                        last = turn(ps[:, j * P:(j + 1) * P], wproj_raw[:, j, k * P:(k + 1) * P])
                    last.then_inc(full(("wpT", k)), 1)

            def drained_by(key):
                await_read(pe, key)

            def outer(b, i):
                t = b * TB + i
                drained_by(("kv", b, i))
                for k in range(KC):
                    if i == 0:
                        wait(pe, drained[6 + k], use[("vk", b, k)][1] - 1)
                    last = mm(of(("vk", b, k))[:, 0:HH * VE], kk[:, t % 2, k * P:(k + 1) * P],
                              vv[:, t % 2, k * HH:(k + 1) * HH, :], start=i == 0, stop=i == TB - 1)
                    if i == TB - 1:
                        last.then_inc(full(("vk", b, k)), 1)
                if i < TB - 1:
                    last.then_inc(kv_used, 1)

            def tokens(b, g):
                keys = [("hT", b, g, k) for k in range(KC)]
                for k in range(KC):
                    fill(pe, keys[k])
                for i in range(GT):
                    t = b * TB + g * GT + i
                    pe.wait_ge(xn_ready, t + 1)
                    for k in range(KC):
                        last = turn(of(keys[k])[:, i * P:(i + 1) * P], xn[:, t, k * P:(k + 1) * P])
                        if i == GT - 1:
                            last.then_inc(full(keys[k]), 1)

            def queries(b, g, m):
                for k in range(KC):
                    drained_by(("hT", b, g, k))
                key = ("q", b, g, m)
                ps = fill(pe, key)
                if b == 0 and g == 0 and m == 0:
                    drained_by(("wT", 2 * KC - 1))
                    drained_by(("wT", 2 * KC - 2))
                for k in range(KC):
                    last = mm(ps[:, :], wT[:, k, m * P:(m + 1) * P], hT[:, k, :], start=k == 0, stop=k == KC - 1)
                last.then_inc(full(key), 1)

            def head(b, g):
                tokens(b, g)
                for m in range(KC):
                    queries(b, g, m)

            def tile(b, i):
                key = ("kv", b, i)
                ps = fill(pe, key)
                a = (i % GT) * P
                for k in range(KC):
                    last = mm(ps[:, :], hT[:, k, a:a + P], wT[:, k, C:3 * C], start=k == 0, stop=k == KC - 1)
                last.then_inc(full(key), 1)
                if i % GT > 0:
                    outer(b, i - 1)

            def tiles(b, g):
                for i in range(g * GT, (g + 1) * GT):
                    tile(b, i)
                outer(b, (g + 1) * GT - 1)

            def attend(b):
                for k in range(KC):
                    drained_by(("vk", b, k))
                drained_by(("q", b, NG - 1, KC - 1))
                for i in range(TB + 2):
                    if i < TB:
                        key = ("o", b, i)
                        ps = fill(pe, key)
                        for k in range(KC):
                            last = mm(ps[:, k * HH * VE:(k + 1) * HH * VE], qT[:, k, i * P:(i + 1) * P], nd[:, k, :],
                                      start=True, stop=True)
                        last.then_inc(full(key), 1)
                    if 1 <= i <= TB:
                        key = ("oT", b, i - 1)
                        drained_by(("o", b, i - 1))
                        ps = fill(pe, key)
                        for k in range(KC):
                            last = turn(ps[:, k * P:(k + 1) * P], o[:, (i - 1) % 2, k * P:(k + 1) * P])
                        last.then_inc(full(key), 1)
                    if b == 0:
                        beside(i)
                    if i >= 2:
                        key = ("proj", b, i - 2)
                        drained_by(("oT", b, i - 2))
                        if b == 0 and i == 2:
                            pe.wait_ge(wpT_ready, 1)
                        ps = fill(pe, key)
                        for k in range(KC):
                            last = mm(ps[:, 0:C], oT[:, i % 2, k, :], wpT[:, b, k, :], start=k == 0, stop=k == KC - 1)
                        last.then_inc(full(key), 1)

            def beside(i):
                if i == 2:
                    tokens(1, 0)
                if i == 4:
                    queries(1, 0, 0)
                if i == 6:
                    queries(1, 0, 1)

            def turn_h2(b, g):
                keys = [("h2T", b, g, k) for k in range(KC)]
                for k in range(KC):
                    fill(pe, keys[k])
                for i in range(GT):
                    pe.wait_ge(h2_ready, b * TB + g * GT + i + 1)
                    for k in range(KC):
                        last = turn(of(keys[k])[:, i * P:(i + 1) * P], h2[:, g * GT + i, k * P:(k + 1) * P])
                        if i == GT - 1:
                            last.then_inc(full(keys[k]), 1)

            def route(b, g):
                key = ("router", b)
                if g == 0:
                    fill(pe, key)
                    if b == 0:
                        pe.wait_ge(ld_route, 32)
                for k in range(KC):
                    drained_by(("h2T", b, g, k))
                for i in range(g * GT, (g + 1) * GT):
                    for k in range(KC):
                        last = mm(of(key)[:, i * E:(i + 1) * E], h2T[:, b, k, i * P:(i + 1) * P], router[:, k, :],
                                  start=k == 0, stop=k == KC - 1)
                if g == NG - 1:
                    last.then_inc(full(key), 1)

            def ranks(b):
                pe.wait_ge(sel_ready, b + 1)
                ps = fill(pe, ("ranks", b))
                w = TB * E
                for k in range(TOPK):
                    mm(ps[:, 0:w], tri[:, :], chosen[:, :, k, :], start=k == 0, stop=k == TOPK - 1)
                for k in range(TOPK):
                    last = mm(ps[:, w:2 * w], ones_bf[:, :], chosen[:, :, k, :].rearrange("p i e -> p e i"),
                              start=k == 0, stop=k == TOPK - 1)
                last.then_inc(full(("ranks", b)), 1)

            def hidden(b, g):
                if b == 0 and g == 0:
                    pe.wait_ge(ld_sh, 16 * (2 + len(SC)))
                for m, (a, n) in enumerate(SC):
                    for s, name in enumerate(("sg", "su")):
                        key = (name, b, g, m)
                        ps = fill(pe, key)
                        for k in range(KC):
                            last = mm(ps[0:n, :], sh_gu[:, s, k, a:a + n], h2T[:, b, k, g * W:(g + 1) * W],
                                      start=k == 0, stop=k == KC - 1)
                        last.then_inc(full(key), 1)

            def shared_rows(b, g):
                for i in range(GT):
                    key = ("sd", b, g * GT + i)
                    ps = fill(pe, key)
                    for m, (a, n) in enumerate(SC):
                        if i == 0:
                            drained_by(("su", b, g, m))
                        last = mm(ps[:, 0:C], sT[0:n, m, i * P:(i + 1) * P], sh_dn[0:n, m, :],
                                  start=m == 0, stop=m == len(SC) - 1)
                    last.then_inc(full(key), 1)

            head(0, 0)
            tiles(0, 0)
            tokens(0, 1)
            modulation(0)
            for m in range(KC):
                queries(0, 1, m)
            for i in range(GT, TB):
                tile(0, i)
                if i == TB - 3:
                    modulation(1)
                if i == TB - 2:
                    projection()
            outer(0, TB - 1)
            attend(0)
            turn_h2(0, 0)
            route(0, 0)
            for i in range(GT):
                if i == GT // 2:
                    turn_h2(0, 1)
                    route(0, 1)
                tile(1, i)
            outer(1, GT - 1)
            head(1, 1)
            ranks(0)
            tiles(1, 1)
            attend(1)
            for g in range(NG):
                turn_h2(1, g)
                route(1, g)
            hidden(0, 0)
            ranks(1)
            shared_rows(0, 0)
            hidden(0, 1)
            shared_rows(0, 1)
            pe.wait_ge(mapf_ready, 1)
            ps = fill(pe, ("map",))
            for a in range(2):
                last = mm(ps[0:1, a * P:(a + 1) * P], mapf[:, a:a + 1], ident[:, :], start=True, stop=True)
            last.then_inc(full(("map",)), 1)
            for g in range(NG):
                hidden(1, g)
                shared_rows(1, g)

            for bank in range(8):
                pe.wait_ge(drained[bank], uses[bank])
            pe.wait_ge(ld_early, 16 * EARLY // 8 * 2 * KC)
            pe.wait_ge(ld_late, 16 * (2 + 2 * KC))

            def turn_x(s, n, turn):
                pe.wait_ge(gathered[s], 16 * (turn + 1))
                wait(pe, xT_copied, n)
                for k in range(KC):
                    last = nc.tensor.transpose(banks[0][:, k * P:(k + 1) * P], xg[:, s, k * P:(k + 1) * P], ident[:, :])
                last.then_inc(x_turned, 1)

            def gate_and_up(c, n, e):
                pe.wait_ge(xT_copied, n + 1)
                for k in range(KC):
                    last = mm(banks[1 + c % 2][:, 0:M2], xT[:, c % 2, k, :],
                              gate_up[:, bass.ds(e * (KC * M2) + k * M2, M2)], start=k == 0, stop=k == KC - 1)
                last.then_inc(gu_done, 1)

            def turn_act(c, n):
                pe.wait_ge(act_done, n + 1)
                wait(pe, aT_copied, n)
                for m in range(2):
                    last = nc.tensor.transpose(banks[3][0:KD, m * P:(m + 1) * P], act[:, c % 2, m * KD:(m + 1) * KD], ident[:, :])
                last.then_inc(act_turned, 1)

            def down_rows(c, n, e):
                pe.wait_ge(aT_copied, n + 1)
                wait(pe, y_scaled, n - 1)
                for m in range(2):
                    last = mm(banks[4 + c % 2][:, 0:C], aT[0:KD, c % 2, m, :],
                              down[0:KD, bass.ds(e * C + m * E * C, C)], start=m == 0, stop=m == 1)
                last.then_inc(y_done, 1)

            PE = mybir.EngineType.PE
            experts = load_values(pe, PE, 0, 0, 0)
            for c in range(2):
                turn_x(c, c, 0)
            for c in range(2):
                gate_and_up(c, c, experts[c])

            def step(turn, last):
                experts = load_values(pe, PE, 0, turn, -1)
                for c in range(R):
                    n = R * turn + c
                    if not last or c + 2 < R:
                        turn_x((c + 2) % R, n + 2, turn + (c + 2) // R)
                    turn_act(c, n)
                    if not first(n):
                        down_rows((c - 1) % R, n - 1, experts[c])
                    if not last or c + 2 < R:
                        gate_and_up(c, n + 2, experts[c + 3])
                    if last and c == R - 1:
                        down_rows(c, n, experts[c + 1])

            blocks(pe, step)


_INS = ['L0_attn_x', 'L0_attn_w_qkv', 'L0_attn_w_proj', 'L0_attn_b_proj', 'L0_ffn_w_router', 'L0_ffn_corr_bias',
        'L0_ffn_gate_w', 'L0_ffn_up_w', 'L0_ffn_down_w', 'L0_ffn_sh_gate_w', 'L0_ffn_sh_up_w', 'L0_ffn_sh_down_w',
        'L0_c', 'L0_wmod']


def kernel(**inputs):
    import numpy as _np
    import concourse.bacc as _bacc
    from concourse import mybir as _mybir
    from concourse.bass_utils import run_bass_kernel_spmd as _run

    nc = _bacc.Bacc("TRN2", target_bir_lowering=False, num_devices=1)
    arrays, args = {}, []
    for name in _INS:
        a = _np.ascontiguousarray(inputs[name])
        arrays[f"in_{name}"] = a
        args.append(nc.dram_tensor(f"in_{name}", a.shape, _mybir.dt.from_np(a.dtype), kind="ExternalInput").ap())
    shape = inputs["L0_attn_x"].shape
    args.append(nc.dram_tensor("out_0", shape, _mybir.dt.float32, kind="ExternalOutput").ap())
    build_block(nc, *args)
    r = _run(nc, [arrays], core_ids=[0])
    return r.results[0]["out_0"]
```
